# Optimizing a Trainium2 kernel written in Bass

```python
import numpy as np
import jax
import jax.numpy as jnp

def _softmax(x, axis=-1):
    return jax.nn.softmax(x, axis=axis)

def _gelu(x):
    return jax.nn.gelu(x, approximate=True)

def _silu(x):
    return jax.nn.silu(x)

def _sigmoid(x):
    return jax.nn.sigmoid(x)

def _layernorm(x, axis=-1, eps=1e-05):
    m = jnp.mean(x, axis=axis, keepdims=True)
    v = jnp.var(x, axis=axis, keepdims=True)
    return (x - m) / jnp.sqrt(v + eps)

def _scatter_add(tgt, idx, src, axis=0):
    return tgt.at[idx].add(src)

def _segment_sum(src, seg, n):
    return jax.ops.segment_sum(src, seg, n)
kernel_name = 'mk_xattn_ffn_d1_seqx_r8_4ef74f'

def setup_inputs(seed: int=0):
    np.random.seed(seed)
    _w = jnp.asarray

    def _rec_inputs():
        import jax
        import jax.numpy as jnp
        _rk = jax.random.key(seed)
        x = -0.0002928 + 1 * jax.random.normal(jax.random.fold_in(_rk, 1), (32, 128, 128), jnp.float32)
        _lenS = 128 - jax.random.randint(jax.random.fold_in(_rk, 7), (32,), 0, max(1, 128 // 4) + 1, jnp.int32)
        _lenS2 = 128 - jax.random.randint(jax.random.fold_in(_rk, 8), (32,), 0, max(1, 128 // 4) + 1, jnp.int32)
        _ctx_1024P = jax.random.normal(jax.random.fold_in(_rk, 11), (32, 16, 128), jnp.float32)
        _ctx_1024c = jax.random.dirichlet(jax.random.fold_in(_rk, 511), 0.3 * jnp.ones((16,), jnp.float32), (32, 128))
        _ctx_1024t = jnp.einsum('bsk,bkd->bsd', _ctx_1024c, _ctx_1024P)
        _ctx_1024t = _ctx_1024t * jax.lax.rsqrt(jnp.mean(jnp.square(_ctx_1024t)) + 1e-12) * 0.953939
        ctx_1024 = -1.39393e-06 + 0.999914 * (_ctx_1024t + 0.3 * jax.random.normal(jax.random.fold_in(_rk, 611), (32, 128, 128), jnp.float32))
        _validS = jnp.arange(128)[None, :] < _lenS[:, None]
        _validS2 = jnp.arange(128)[None, :] < _lenS2[:, None]
        _causal = jnp.tril(jnp.ones((128, 128), dtype=bool))
        mask_BxS2_bf1 = jnp.ones((32, 128), dtype=bool)
        return (x, ctx_1024, mask_BxS2_bf1)
    x, ctx_1024, mask_BxS2_bf1 = _rec_inputs()

    def _L0_xattn_setup():
        import jax, jax.numpy as jnp
        import numpy as np
        B, TQ, TKV, C, H = (2, 256, 256, 128, 16)
        HD = C // H
        key = jax.random.key(seed)
        k1, k2, k3, k4, k5 = jax.random.split(key, 5)
        scale = 0.02
        return {'x_q': jax.random.normal(k1, (B, TQ, C), jnp.float32), 'x_kv': jax.random.normal(k2, (B, TKV, C), jnp.float32), 'q_tok_mask': jnp.ones((B, TQ), dtype=bool), 'kv_tok_mask': jnp.ones((B, TKV), dtype=bool), 'Wq': jax.random.normal(k3, (C, C), jnp.float32) * scale, 'Wkv': jax.random.normal(k4, (2 * C, C), jnp.float32) * scale, 'Wc': jax.random.normal(k5, (C, C), jnp.float32) * scale}
    _L0_xattn_all = _L0_xattn_setup()
    _L0_xattn_in = {k: v for k, v in _L0_xattn_all.items() if k in ('Wq', 'Wkv', 'Wc')}
    del _L0_xattn_all

    def _L0_ffn_setup():
        import jax, jax.numpy as jnp
        import numpy as np
        D = 128
        F = 512
        E = 8
        K = 2
        B, S = (4, 256)
        key = jax.random.key(seed)
        ks = jax.random.split(key, 6)
        scale_in = 1.0 / np.sqrt(D)
        scale_mid = 1.0 / np.sqrt(F)
        return {'x': jax.random.normal(ks[0], (B, S, D), dtype=jnp.float32), 'router_w': jax.random.normal(ks[1], (E, D), dtype=jnp.float32) * scale_in, 'w1': jax.random.normal(ks[2], (E, F, D), dtype=jnp.float32) * scale_in, 'b1': jax.random.normal(ks[3], (E, F), dtype=jnp.float32) * 0.01, 'w2': jax.random.normal(ks[4], (E, D, F), dtype=jnp.float32) * scale_mid, 'b2': jax.random.normal(ks[5], (E, D), dtype=jnp.float32) * 0.01}
    _L0_ffn_all = _L0_ffn_setup()
    _L0_ffn_in = {k: v for k, v in _L0_ffn_all.items() if k in ('router_w', 'w1', 'b1', 'w2', 'b2')}
    del _L0_ffn_all
    return {'x': x, 'ctx_1024': ctx_1024, 'mask_BxS2_bf1': mask_BxS2_bf1, 'L0_xattn_Wq': _L0_xattn_in['Wq'], 'L0_xattn_Wkv': _L0_xattn_in['Wkv'], 'L0_xattn_Wc': _L0_xattn_in['Wc'], 'L0_ffn_router_w': _L0_ffn_in['router_w'], 'L0_ffn_w1': _L0_ffn_in['w1'], 'L0_ffn_b1': _L0_ffn_in['b1'], 'L0_ffn_w2': _L0_ffn_in['w2'], 'L0_ffn_b2': _L0_ffn_in['b2']}

def reference(x, ctx_1024, mask_BxS2_bf1, L0_xattn_Wq, L0_xattn_Wkv, L0_xattn_Wc, L0_ffn_router_w, L0_ffn_w1, L0_ffn_b1, L0_ffn_w2, L0_ffn_b2):
    import jax
    import jax.numpy as jnp

    def _L0_xattn_ref(x_q, x_kv, q_tok_mask, kv_tok_mask, Wq, Wkv, Wc):
        import jax, jax.numpy as jnp
        import numpy as np
        B, TQ, TKV, C, H = (2, 256, 256, 128, 16)
        HD = C // H
        b, tq, c = x_q.shape
        tkv = x_kv.shape[1]
        q = (x_q @ Wq.T).reshape(b, tq, H, HD).transpose(0, 2, 1, 3)
        kv = x_kv @ Wkv.T
        k, v = (kv[..., :c], kv[..., c:])
        k = k.reshape(b, tkv, H, HD).transpose(0, 2, 1, 3)
        v = v.reshape(b, tkv, H, HD).transpose(0, 2, 1, 3)
        scores = jnp.einsum('bhqd,bhkd->bhqk', q, k) / jnp.sqrt(jnp.float32(HD))
        mask = (q_tok_mask[:, :, None] & kv_tok_mask[:, None, :])[:, None]
        scores = jnp.where(mask, scores, jnp.float32(-1000000000.0))
        att = jax.nn.softmax(scores, axis=-1)
        y = jnp.einsum('bhqk,bhkd->bhqd', att, v)
        y = y.transpose(0, 2, 1, 3).reshape(b, tq, c)
        return y @ Wc.T

    def _L0_ffn_ref(x, router_w, w1, b1, w2, b2):
        import jax, jax.numpy as jnp
        import numpy as np
        D = 128
        F = 512
        E = 8
        K = 2
        B, S = (4, 256)
        orig_shape = x.shape
        xf = x.reshape(-1, D)
        logits = jnp.einsum('td,ed->te', xf, router_w)
        top_vals, top_idx = jax.lax.top_k(logits, K)
        probs = jax.nn.softmax(top_vals, axis=-1)
        out = jnp.zeros_like(xf)
        for e in range(E):
            w = jnp.sum(jnp.where(top_idx == e, probs, 0.0), axis=-1)
            h = jax.nn.gelu(jnp.einsum('td,fd->tf', xf, w1[e]) + b1[e], approximate=False)
            y = jnp.einsum('tf,df->td', h, w2[e]) + b2[e]
            out = out + w[:, None] * y
        return out.reshape(orig_shape)
    x = x + _L0_xattn_ref(_layernorm(x, axis=-1), ctx_1024, mask_BxS2_bf1, mask_BxS2_bf1, L0_xattn_Wq, L0_xattn_Wkv, L0_xattn_Wc)
    x = x + _L0_ffn_ref(_layernorm(x, axis=-1), L0_ffn_router_w, L0_ffn_w1, L0_ffn_b1, L0_ffn_w2, L0_ffn_b2)
    return x

_drawn_inputs = setup_inputs


def setup_inputs(seed=0):
    import zlib

    import numpy as np

    out = dict(_drawn_inputs(seed))
    spreads = {}
    factors = {'L0_xattn_Wq': 18.569, 'L0_ffn_b1': 8.0, 'L0_ffn_b2': 8.0}
    for name, (base, spread) in spreads.items():
        noise = np.random.default_rng([zlib.crc32(name.encode()), seed]).standard_normal(out[name].shape)
        drawn = base * np.exp(spread * noise) if base else spread * noise
        out[name] = jnp.asarray(drawn.astype(out[name].dtype))
    for name, factor in factors.items():
        out[name] = (out[name] * factor).astype(out[name].dtype)
    return out
```

```python
from contextlib import ExitStack

import concourse.bass as bass
from concourse import mybir

F32 = mybir.dt.float32
BF16 = mybir.dt.bfloat16
U8 = mybir.dt.uint8
ALU = mybir.AluOpType
ACT = mybir.ActivationFunctionType
AX = mybir.AxisListType

P = 128
BATCH, SEQ, D = 32, 128, 128
HEADS = 16
HD = D // HEADS
PAIRS = HEADS // 2
GB = 4
GROUPS = BATCH // GB
GT = GB * SEQ
EPS = 1e-5
EXPERTS, FF = 8, 512
FC = FF // P
HALF = P // 2
SIDE_ROW = 6 * HD
SHIFT_ROW = SIDE_ROW + 3
Q_PARTS = (0, 0, 1, 1, 0, 2)
K_PARTS = (0, 1, 0, 1, 2, 0)
UNITS = HEADS // 4
UW = 4 * SEQ
ROUTER_STEPS = 19
CREDIT = 1
S1_SPREAD = (6, 5, 5, 0)


def bf16_parts(value):
    import numpy as np
    rest, parts = np.float32(value), []
    for _ in range(3):
        bits = np.array(rest, np.float32).view(np.uint32)
        top = np.array((int(bits) & 0xFFFF0000), np.uint32).view(np.float32)
        parts.append(float(top))
        rest = np.float32(rest - top)
    return parts


def xattn_ffn(nc, x, ctx_t, mask, mask_t, wq_t, wkv_t, wc_t, router_t, w1_t, b1_t, w2_t, b2, out):
    stack = ExitStack()
    with stack:
        def sb(name, shape, dt=F32):
            return stack.enter_context(nc.sbuf_tensor(name, shape, dt))

        def ps(name, shape, dt=F32):
            return stack.enter_context(nc.psum_tensor(name, shape, dt))

        def sem(name):
            return stack.enter_context(nc.semaphore(name))

        xs = sb("xs", [P, BATCH, D])
        mask_rows8 = sb("mask_rows8", [GROUPS, GT], U8)
        mask_rows = sb("mask_rows", [GROUPS, GT], BF16)
        key_terms = sb("key_terms", [GROUPS, 6, GT], BF16)
        query_terms = sb("query_terms", [GROUPS, 6, GT], BF16)
        mask_cols8 = sb("mask_cols8", [P, BATCH], U8)
        mask_cols = sb("mask_cols", [P, BATCH])
        wq_sb = sb("wq_sb", [P, D])
        wkv_sb = sb("wkv_sb", [P, 2 * D])
        wc_sb = sb("wc_sb", [P, D])
        ident = sb("ident", [P, P])
        ident_b = sb("ident_b", [P, P], BF16)
        ctx_sb = [sb(f"ctx{i}", [P, GT]) for i in range(2)]
        kmask = [sb(f"kmask{i}", [P, GT], BF16) for i in range(2)]
        stats = sb("stats", [P, GB, 6])
        mean = sb("mean", [P, GB])
        ln_tmp = sb("ln_tmp", [P, 4, GB])
        var_eps = sb("var_eps", [P, GB])
        minus_half = sb("minus_half", [P, GB])
        zero = sb("zero", [P, 1])
        rstd = sb("rstd", [P, GB])
        qscale = sb("qscale", [P, GB])
        xq = sb("xq", [P, GB, D])
        xq_t = sb("xq_t", [P, GT])
        q32 = sb("q32", [P, GT])
        k32 = sb("k32", [P, GT])
        qpart = [sb(f"qpart{i}", [P, GT], BF16) for i in range(3)]
        kpart = [sb(f"kpart{i}", [P, GT], BF16) for i in range(3)]
        qrest = sb("qrest", [P, GT])
        krest = sb("krest", [P, GT])
        qstack = [sb(f"qstack{i}", [P, 2, PAIRS, GT], BF16) for i in range(2)]
        kstack = [sb(f"kstack{i}", [P, PAIRS, GT], BF16) for i in range(2)]
        negmax = sb("negmax", [P, 2, PAIRS, GB])
        shift = sb("shift", [P, 2, 3, PAIRS * GB], BF16)
        shift_rest = sb("shift_rest", [P, 2, PAIRS * GB])
        shift_t = sb("shift_t", [3 * PAIRS * GB, 2, SEQ], BF16)
        probs = [sb(f"probs{i}", [P, HEADS * SEQ]) for i in range(2)]
        values = [sb(f"values{i}", [P, GB, HEADS, HD + 1]) for i in range(2)]
        denom = sb("denom", [P, HEADS])
        y = sb("y", [P, HEADS, HD])
        y_t = sb("y_t", [P, SEQ])

        router_sb = sb("router_sb", [P, EXPERTS])
        w1_sb = sb("w1_sb", [P, EXPERTS, FF])
        w2_sb = sb("w2_sb", [P, EXPERTS, FC, D])
        b1_sb = sb("b1_sb", [P, EXPERTS, FC])
        b2_sb = sb("b2_sb", [EXPERTS, D])
        iota_i = sb("iota_i", [P, EXPERTS], mybir.dt.int32)
        iota8 = sb("iota8", [P, EXPERTS])
        logits = sb("logits", [P, GB, EXPERTS])
        chosen = [sb(f"chosen{i}", [P, GB, EXPERTS]) for i in range(2)]
        tmp8 = sb("tmp8", [P, GB, EXPERTS])
        masked = sb("masked", [P, GB, EXPERTS])
        top = [sb(f"top{i}", [P, GB]) for i in range(2)]
        index = sb("index", [P, GB])
        gap = sb("gap", [P, GB])
        ratio = sb("ratio", [P, GB])
        share = [sb(f"share{i}", [P, GB]) for i in range(2)]
        gate = sb("gate", [P, GB, EXPERTS])
        gate_t = sb("gate_t", [EXPERTS, GT])
        hidden = [sb(f"hidden{i}", [P, FC, GT]) for i in range(2)]

        smax = [ps(f"smax{i}", [P, 2, 2, SEQ]) for i in range(2)]
        sexp = [ps(f"sexp{i}", [P, 4, 2, SEQ]) for i in range(2)]
        prep = ps("prep", [P, GT])
        tail = ps("tail", [P, GT])
        shift_ps = prep[:].bitcast(BF16)
        attn_ps = tail[:, 0:HEADS * (HD + 1)].rearrange("p (h c) -> p h c", c=HD + 1)

        key_terms_d = nc.dram_tensor("key_terms_d", [GROUPS, 6, GT], BF16, kind="Internal").ap()
        query_terms_d = nc.dram_tensor("query_terms_d", [GROUPS, 6, GT], BF16, kind="Internal").ap()
        mask_d = nc.dram_tensor("mask_d", [GROUPS, GT], BF16, kind="Internal").ap()

        x_loaded = sem("x_loaded")
        weights_loaded = sem("weights_loaded")
        masks_loaded = sem("masks_loaded")
        terms_stored = sem("terms_stored")
        ctx_loaded = [sem(f"ctx_loaded{i}") for i in range(2)]
        stacks_loaded = [sem(f"stacks_loaded{i}") for i in range(2)]
        shift_loaded = sem("shift_loaded")
        ident_zero = sem("ident_zero")
        ident_made = sem("ident_made")
        cleared = sem("cleared")
        values_set = sem("values_set")
        mask_prep = sem("mask_prep")
        ln_stats = sem("ln_stats")
        ln_moments = sem("ln_moments")
        ln_var = sem("ln_var")
        ln_rstd = sem("ln_rstd")
        ln_scale = sem("ln_scale")
        xq_ready = sem("xq_ready")
        xqt_done = sem("xqt_done")
        xqt_copied = sem("xqt_copied")
        q_done = sem("q_done")
        q_copied = sem("q_copied")
        k_done = sem("k_done")
        k_masked = sem("k_masked")
        v_done = sem("v_done")
        v_copied = sem("v_copied")
        q_split = sem("q_split")
        k_split = sem("k_split")
        smax_done = sem("smax_done")
        max_taken = sem("max_taken")
        shift_split = sem("shift_split")
        shift_turned = sem("shift_turned")
        shift_copied = sem("shift_copied")
        sexp_done = sem("sexp_done")
        exp_done = sem("exp_done")
        attn_done = sem("attn_done")
        denom_done = sem("denom_done")
        y_ready = sem("y_ready")
        yt_done = sem("yt_done")
        yt_copied = sem("yt_copied")
        proj_done = sem("proj_done")
        resid_done = sem("resid_done")
        out_stored = sem("out_stored")
        router_steps = sem("router_steps")
        ratio_done = sem("ratio_done")
        logits_done = sem("logits_done")
        gate_done = sem("gate_done")
        gate_copied = sem("gate_copied")
        bias_done = sem("bias_done")
        hidden_done = sem("hidden_done")
        gelu_done = sem("gelu_done")
        expert_done = sem("expert_done")
        expert_added = sem("expert_added")
        ffn_loaded = sem("ffn_loaded")

        STACK_DMAS = 2 * 2 * len(Q_PARTS) + 4
        neg = bf16_parts(-1e9)

        def stacks_ready(eng, g, gp):
            eng.wait_ge(stacks_loaded[gp], 16 * STACK_DMAS * ((g - gp) // 2 + 1))

        hidden_ps = [sexp[i][:].rearrange("p i h q -> p (i h q)")[:, k * GT:(k + 1) * GT] for i in range(2) for k in range(2)]
        expert_ps = [smax[i][:].rearrange("p i h q -> p (i h) q") for i in range(2)]
        block = stack.enter_context(nc.Block())

        @block.sync
        def _(sp):
            sp.dma_start(mask_rows8[:], mask).then_inc(masks_loaded, 16)
            sp.dma_start(mask_cols8[:], mask_t).then_inc(masks_loaded, 16)

            sp.dma_start(xs[:, 0:GB, :], x[:, 0:GB, :]).then_inc(x_loaded, 16)
            sp.dma_start(xs[:, GB:, :], x[:, GB:, :]).then_inc(x_loaded, 16)
            sp.dma_start(wq_sb[:], wq_t).then_inc(weights_loaded, 16)
            sp.dma_start(wkv_sb[:], wkv_t).then_inc(weights_loaded, 16)
            sp.dma_start(wc_sb[:], wc_t).then_inc(weights_loaded, 16)
            for dst, src in ((router_sb, router_t), (w1_sb, w1_t), (w2_sb, w2_t), (b1_sb, b1_t), (b2_sb, b2)):
                sp.dma_start(dst[:], src).then_inc(ffn_loaded, 16)
            sp.wait_ge(mask_prep, 10)
            sp.dma_start(key_terms_d, key_terms[:]).then_inc(terms_stored, 16)
            sp.dma_start(query_terms_d, query_terms[:]).then_inc(terms_stored, 16)
            sp.dma_start(mask_d, mask_rows[:]).then_inc(terms_stored, 16)
            sp.wait_ge(terms_stored, 48)

            def load_ctx(g, gp):
                sp.dma_start(ctx_sb[gp][:], ctx_t[:, bass.ds(g * GT, GT)]).then_inc(ctx_loaded[gp], 16)
                sp.dma_start(kmask[gp][:], mask_d[bass.ds(g, 1), :].to_broadcast([P, GT])).then_inc(ctx_loaded[gp], 16)

            def stack_side(gp, side, parts, tile, hp):
                for slot, part in enumerate(side):
                    row = HALF * hp + HD * slot
                    dst = tile[row:row + HD, :, :]
                    sp.dma_start(dst, parts[part][HALF * hp:HALF * (hp + 1), :]).then_inc(stacks_loaded[gp], 16)

            def load_stacks(g, gp, reuse):
                if reuse:
                    sp.wait_ge(sexp_done, 8 * (g - 1))
                for hp in range(2):
                    row = HALF * hp + SIDE_ROW
                    for tile, terms in ((kstack[gp][row:row + 6, :, :], key_terms_d),
                                        (qstack[gp][row:row + 6, hp, :, :], query_terms_d)):
                        src = terms[bass.ds(g, 1), :, :].rearrange("g s t -> (g s) t").rearrange("s (o t) -> s o t", o=1)
                        sp.dma_start(tile, src.to_broadcast([6, PAIRS, GT])).then_inc(stacks_loaded[gp], 16)
                sp.wait_ge(k_split, 4 * (g + 1))
                for hp in range(2):
                    stack_side(gp, K_PARTS, kpart, kstack[gp], hp)
                sp.wait_ge(q_split, 4 * (g + 1))
                for hp in range(2):
                    stack_side(gp, Q_PARTS, qpart, qstack[gp][:, hp, :, :], hp)

            def load_shift(g, gp):
                sp.wait_ge(shift_copied, g + 1)
                for hp in range(2):
                    row = HALF * hp + SHIFT_ROW
                    sp.dma_start(qstack[gp][row:row + 3, hp, :, :].rearrange("s i t -> s (i t)"),
                                 shift_t[:, hp, :]).then_inc(shift_loaded, 16)

            load_ctx(0, 0)
            load_ctx(1, 1)
            sp.wait_ge(cleared, 4)
            load_stacks(0, 0, False)
            load_stacks(1, 1, False)
            load_shift(0, 0)

            def group(g, gp, next_group, second_next):
                if second_next:
                    sp.wait_ge(v_copied, g + 1)
                    load_ctx(g + 2, gp)
                if next_group:
                    load_shift_first = True
                if second_next:
                    load_stacks(g + 2, gp, True)
                if next_group:
                    load_shift(g + 1, 1 - gp)

            with sp.Fori(0, GROUPS // 2 - 1) as it:
                for gp in range(2):
                    group(2 * it + gp, gp, True, True)
            group(GROUPS - 2, 0, True, False)
            sp.wait_ge(expert_added, GROUPS * (EXPERTS + 1) * GB)
            sp.dma_start(out, xs[:]).then_inc(out_stored, 16)
            sp.wait_ge(out_stored, 16)

        @block.gpsimd
        def _(pool):
            nc.gpsimd.memset(ident[:], 0.0).then_inc(ident_zero, 1)
            nc.gpsimd.memset(ident_b[:], 0.0).then_inc(ident_zero, 1)
            pool.wait_ge(ident_zero, 2)
            for m in (ident, ident_b):
                nc.gpsimd.affine_select(out=m[:], in_=m[:], compare_op=ALU.not_equal, fill=1.0, base=0,
                                        pattern=[[-1, P]], channel_multiplier=1).then_inc(ident_made, 1)
            nc.gpsimd.iota(iota_i[:], [[1, EXPERTS]], base=EXPERTS, channel_multiplier=0).then_inc(ident_made, 1)
            nc.gpsimd.memset(minus_half[:], -0.5).then_inc(ident_made, 1)
            nc.gpsimd.memset(zero[:], 0.0).then_inc(ident_made, 1)
            pool.wait_ge(ident_made, 5)
            for i in range(2):
                nc.gpsimd.memset(values[i][:], 1.0).then_inc(values_set, 1)

            no_shift = zero[:].to_broadcast([P, GT])

            def split(g, src, parts, rest, src_ready, step):
                pool.wait_ge(src_ready, g + 1)
                nc.gpsimd.tensor_tensor(parts[0][:], src[:], no_shift, ALU.add).then_inc(step, 1)
                pool.wait_ge(step, 4 * g + 1)
                nc.gpsimd.tensor_tensor(rest[:], src[:], parts[0][:], ALU.subtract).then_inc(step, 1)
                pool.wait_ge(step, 4 * g + 2)
                nc.gpsimd.tensor_tensor(parts[1][:], rest[:], no_shift, ALU.add).then_inc(step, 1)
                pool.wait_ge(step, 4 * g + 3)
                nc.gpsimd.tensor_tensor(parts[2][:], rest[:], parts[1][:], ALU.subtract).then_inc(step, 1)

            def splits(g, reuse):
                pool.wait_ge(ln_var, g + 1)
                nc.gpsimd.tensor_tensor(rstd[:], var_eps[:], minus_half[:], ALU.pow).then_inc(ln_rstd, 1)
                if reuse:
                    stacks_ready(pool, g - 1, reuse - 1)
                split(g, k32, kpart, krest, k_masked, k_split)
                split(g, q32, qpart, qrest, q_copied, q_split)

            splits(0, 0)
            splits(1, 1)
            with pool.Fori(0, GROUPS // 2 - 1) as it:
                for gp in range(2):
                    splits(2 * it + gp + 2, 2 - gp)
            with pool.Fori(0, GROUPS) as g:
                pool.wait_ge(ln_var, GROUPS + g + 1)
                nc.gpsimd.tensor_tensor(rstd[:], var_eps[:], minus_half[:], ALU.pow).then_inc(ln_rstd, 1)

        @block.scalar
        def _(act):
            def copy_xqt(g, first=False):
                act.wait_ge(xqt_done, g + 1)
                if not first:
                    act.wait_ge(q_done, g)
                nc.scalar.activation(xq_t[:], prep[:], ACT.Copy).then_inc(xqt_copied, 1)

            def copy_q(g, first=False):
                act.wait_ge(q_done, g + 1)
                if not first:
                    act.wait_ge(q_split, 4 * g)
                nc.scalar.activation(q32[:], prep[:], ACT.Copy).then_inc(q_copied, 1)

            def copy_v(g, gp, first=False):
                act.wait_ge(v_done, g + 1)
                if not first:
                    act.wait_ge(attn_done, 4 * (g - 1) + CREDIT)
                nc.scalar.activation(values[gp][:, :, :, 0:HD],
                                     prep[:].rearrange("p (b h d) -> p b h d", b=GB, d=HD),
                                     ACT.Copy).then_inc(v_copied, 1)

            def copy_shift(g, first=False):
                act.wait_ge(shift_turned, g + 1)
                if not first:
                    act.wait_ge(shift_loaded, 32 * g)
                nc.scalar.activation(shift_t[:], shift_ps[0:3 * PAIRS * GB, 0:2 * SEQ].rearrange("p (h q) -> p h q", h=2),
                                     ACT.Copy).then_inc(shift_copied, 1)

            def exp(n, np_, u, free):
                act.wait_ge(sexp_done, 2 * n + u + 1)
                if free:
                    act.wait_ge(attn_done, n - 1 + CREDIT)
                w = HEADS * SEQ // 2
                nc.scalar.activation(probs[np_][:, u * w:(u + 1) * w],
                                     sexp[u][:].rearrange("p i h q -> p (i h q)"), ACT.Exp).then_inc(exp_done, 1)

            def copy_yt(n, first):
                act.wait_ge(yt_done, n + 1 + CREDIT)
                if not first:
                    act.wait_ge(proj_done, n + CREDIT)
                nc.scalar.activation(y_t[:], tail[:, 0:SEQ], ACT.Copy).then_inc(yt_copied, 1)

            act.wait_ge(values_set, 2)
            for g in range(2):
                copy_xqt(g, g == 0)
                copy_q(g, g == 0)
            copy_v(0, 0, True)
            copy_shift(0, True)
            for u in range(2):
                exp(0, 0, u, False)

            def group(g, gp, next_group, second_next, start=False):
                for b in range(GB):
                    n = GB * g + b
                    last = b == GB - 1 and not next_group
                    if b == GB - 1:
                        if next_group:
                            copy_shift(g + 1)
                        copy_yt(n, False)
                    if not last:
                        exp(n + 1, (b + 1) % 2, 0, True)
                    if b < GB - 1:
                        copy_yt(n, False)
                    if not last:
                        exp(n + 1, (b + 1) % 2, 1, True)
                    if b == 0 and next_group:
                        copy_v(g + 1, 1 - gp, False)
                    if b == 1 and second_next:
                        copy_xqt(g + 2)
                        copy_q(g + 2)

            with act.Fori(0, GROUPS // 2 - 1) as it:
                for gp in range(2):
                    group(2 * it + gp, gp, True, True)
            group(GROUPS - 2, 0, True, False)
            group(GROUPS - 1, 1, False, False)

            with act.Fori(0, GROUPS) as g:
                copy_xqt(g + GROUPS, True)
                act.wait_ge(router_steps, ROUTER_STEPS * g + 10)
                nc.scalar.activation(ratio[:], gap[:], ACT.Exp).then_inc(ratio_done, 1)
                act.wait_ge(gate_done, g + 1)
                nc.scalar.activation(gate_t[:], prep[0:EXPERTS, :], ACT.Copy).then_inc(gate_copied, 1)
                for e in range(EXPERTS):
                    for c in range(FC):
                        m = FC * e + c
                        act.wait_ge(hidden_done, EXPERTS * FC * g + m + 1)
                        if e >= 2:
                            act.wait_ge(expert_done, EXPERTS * g + e - 1)
                        nc.scalar.activation(hidden[e % 2][:, c, :], hidden_ps[m % 4], ACT.Gelu,
                                             bias=b1_sb[:, e, c:c + 1]).then_inc(gelu_done, 1)

        @block.tensor
        def _(pe):
            def turn_xq(g):
                pe.wait_ge(xq_ready, GB * (g + 1))
                for b in range(GB):
                    last = nc.tensor.transpose(prep[:, b * SEQ:(b + 1) * SEQ], xq[:, b, :], ident[:])
                last.then_inc(xqt_done, 1)

            def project_q(g):
                pe.wait_ge(xqt_copied, g + 1)
                nc.tensor.matmul(prep[:], wq_sb[:], xq_t[:], start=True, stop=True).then_inc(q_done, 1)

            def project_k(g, gp):
                pe.wait_ge(ctx_loaded[gp], 32 * ((g - gp) // 2 + 1))
                nc.tensor.matmul(prep[:], wkv_sb[:, 0:D], ctx_sb[gp][:], start=True, stop=True).then_inc(k_done, 1)

            def project_v(g, gp):
                for b in range(GB):
                    last = nc.tensor.matmul(prep[:, b * D:(b + 1) * D], ctx_sb[gp][:, b * SEQ:(b + 1) * SEQ],
                                            wkv_sb[:, D:2 * D], start=True, stop=True)
                last.then_inc(v_done, 1)

            def turn_shift(g):
                pe.wait_ge(shift_split, 4 * (g + 1))
                for hp in range(2):
                    last = nc.tensor.transpose(shift_ps[0:3 * PAIRS * GB, hp * SEQ:(hp + 1) * SEQ],
                                               shift[:, hp, :, :].rearrange("p s c -> p (s c)"), ident_b[:])
                last.then_inc(shift_turned, 1)

            def scores_for_max(g, gp, j, free):
                b, u = divmod(j, UNITS)
                if free:
                    pe.wait_ge(max_taken, 4 * UNITS * g + j - 1)
                ks = slice(b * SEQ, (b + 1) * SEQ)
                for i in range(2):
                    for hp in range(2):
                        last = nc.tensor.matmul(smax[j % 2][:, i, hp, :], qstack[gp][:, hp, 2 * u + i, ks],
                                                kstack[gp][:, 2 * u + i, ks], start=True, stop=True)
                last.then_inc(smax_done, 1)

            def scores_for_exp(n, b, gp, u, free):
                if free:
                    pe.wait_ge(exp_done, 2 * n + u - 1)
                ks = slice(b * SEQ, (b + 1) * SEQ)
                for i in range(4):
                    last = nc.tensor.matmul(sexp[u][:, i, :, :], kstack[gp][:, 4 * u + i, ks],
                                            qstack[gp][:, :, 4 * u + i, ks], start=True, stop=True)
                last.then_inc(sexp_done, 1)

            def attend(n, b, gp, first):
                pe.wait_ge(exp_done, 2 * n + 2)
                if not first:
                    pe.wait_ge(resid_done, n + CREDIT)
                for h in range(HEADS):
                    last = nc.tensor.matmul(attn_ps[:, h, :], probs[b % 2][:, h * SEQ:(h + 1) * SEQ],
                                            values[gp][:, b, h, :], start=True, stop=True)
                last.then_inc(attn_done, 1)

            def turn_y(n):
                pe.wait_ge(y_ready, n + 1)
                nc.tensor.transpose(tail[:, 0:SEQ], y[:].rearrange("p h d -> p (h d)"), ident[:]).then_inc(yt_done, 1)

            def project_y(n):
                pe.wait_ge(yt_copied, n + 1)
                nc.tensor.matmul(tail[:, 0:D], y_t[:], wc_sb[:], start=True, stop=True).then_inc(proj_done, 1)

            for begun in (attn_done, yt_done, proj_done):
                pe.sem_inc(begun, CREDIT)
            pe.wait_ge(weights_loaded, 48)
            pe.wait_ge(ident_made, 2)
            for g in range(2):
                if g:
                    pe.wait_ge(q_copied, g)
                project_k(g, g)
                pe.wait_ge(k_masked, g + 1)
                turn_xq(g)
                project_q(g)
            pe.wait_ge(q_copied, 2)
            project_v(0, 0)
            stacks_ready(pe, 0, 0)
            for j in range(4 * UNITS):
                scores_for_max(0, 0, j, j >= 2)
            pe.wait_ge(v_copied, 1)
            turn_shift(0)
            pe.wait_ge(shift_loaded, 32)
            for u in range(2):
                scores_for_exp(0, 0, 0, u, False)

            def group(g, gp, next_group, second_next, start=False):
                j = 0
                for b in range(GB):
                    n = GB * g + b
                    attend(n, b, gp, start and b == 0)
                    ngp, nb = (gp, b + 1) if b < GB - 1 else (1 - gp, 0)
                    more = b < GB - 1 or next_group
                    if b == GB - 1 and next_group:
                        turn_shift(g + 1)
                    if b < GB - 1:
                        scores_for_exp(n + 1, nb, ngp, 0, True)
                    turn_y(n)
                    if next_group:
                        if b == 0:
                            stacks_ready(pe, g + 1, 1 - gp)
                        for _ in range(S1_SPREAD[b]):
                            scores_for_max(g + 1, 1 - gp, j, True)
                            j += 1
                    if b < GB - 1:
                        scores_for_exp(n + 1, nb, ngp, 1, True)
                    project_y(n)
                    if b == 0 and next_group:
                        pe.wait_ge(shift_copied, g + 1)
                        project_v(g + 1, 1 - gp)
                        if second_next:
                            pe.wait_ge(v_copied, g + 2)
                            project_k(g + 2, gp)
                    if b == 1 and second_next:
                        pe.wait_ge(k_masked, g + 3)
                        turn_xq(g + 2)
                        project_q(g + 2)
                    if b == 2 and next_group:
                        if second_next:
                            pe.wait_ge(q_copied, g + 3)
                        else:
                            pe.wait_ge(v_copied, g + 2)
                    if b == GB - 1 and next_group:
                        pe.wait_ge(shift_loaded, 32 * (g + 2))
                        for u in range(2):
                            scores_for_exp(n + 1, nb, ngp, u, True)

            with pe.Fori(0, GROUPS // 2 - 1) as it:
                for gp in range(2):
                    group(2 * it + gp, gp, True, True)
            group(GROUPS - 2, 0, True, False)
            group(GROUPS - 1, 1, False, False)

            pe.wait_ge(ffn_loaded, 5 * 16)
            with pe.Fori(0, GROUPS) as g:
                turn_xq(g + GROUPS)
                pe.wait_ge(xqt_copied, g + GROUPS + 1)
                for b in range(GB):
                    last = nc.tensor.matmul(tail[:, b * EXPERTS:(b + 1) * EXPERTS], xq_t[:, b * SEQ:(b + 1) * SEQ],
                                            router_sb[:], start=True, stop=True)
                last.then_inc(logits_done, 1)

                def up(e):
                    for c in range(FC):
                        m = FC * e + c
                        if m >= 4:
                            pe.wait_ge(gelu_done, EXPERTS * FC * g + m - 3)
                        nc.tensor.matmul(hidden_ps[m % 4], w1_sb[:, e, c * P:(c + 1) * P], xq_t[:],
                                         start=True, stop=True).then_inc(hidden_done, 1)

                def down(e):
                    pe.wait_ge(gelu_done, EXPERTS * FC * g + FC * (e + 1))
                    if e >= 2:
                        pe.wait_ge(expert_added, (EXPERTS + 1) * GB * g + GB * e)
                    for b in range(GB):
                        for c in range(FC):
                            last = nc.tensor.matmul(expert_ps[e % 2][:, b, :], hidden[e % 2][:, c, b * SEQ:(b + 1) * SEQ],
                                                    w2_sb[:, e, c, :], start=(c == 0), stop=(c == FC - 1))
                    last.then_inc(expert_done, 1)

                up(0)
                pe.wait_ge(router_steps, ROUTER_STEPS * (g + 1) + 1)
                for b in range(GB):
                    last = nc.tensor.transpose(prep[0:EXPERTS, b * SEQ:(b + 1) * SEQ], gate[:, b, :], ident[:])
                last.then_inc(gate_done, 1)
                pe.wait_ge(gate_copied, g + 1)
                for b in range(GB):
                    last = nc.tensor.matmul(tail[:, b * D:(b + 1) * D], gate_t[:, b * SEQ:(b + 1) * SEQ], b2_sb[:],
                                            start=True, stop=True)
                last.then_inc(bias_done, 1)
                for e in range(EXPERTS):
                    if e + 1 < EXPERTS:
                        up(e + 1)
                    down(e)

        @block.vector
        def _(dve):
            steps = [0]

            def step(ins):
                steps[0] += 1
                ins.then_inc(mask_prep, 1)

            dve.sem_inc(resid_done, CREDIT)
            dve.wait_ge(masks_loaded, 32)
            step(nc.vector.tensor_copy(mask_rows[:], mask_rows8[:]))
            step(nc.vector.tensor_scalar(mask_cols[:], mask_cols8[:], float(HD) ** -0.5, None, ALU.mult))
            step(nc.vector.memset(key_terms[:, 3:6, :], 1.0))
            step(nc.vector.memset(query_terms[:, 3:6, :], 0.0))
            dve.wait_ge(mask_prep, 4)
            for s in range(3):
                step(nc.vector.tensor_scalar(key_terms[:, s, :], mask_rows[:], -neg[s], neg[s], ALU.mult, ALU.add))
                step(nc.vector.tensor_copy(query_terms[:, s, :], mask_rows[:]))
            for i in range(2):
                nc.vector.memset(qstack[i][:], 0.0).then_inc(cleared, 1)
                nc.vector.memset(kstack[i][:], 0.0).then_inc(cleared, 1)

            def layernorm_stats(g, done=0):
                for b in range(GB):
                    nc.vector.bn_stats(stats[:, b, :], xs[:, GB * g + b, :]).then_inc(ln_stats, 1)
                dve.wait_ge(ln_stats, GB * (g + done + 1))
                mean_sum, mean_diff, moment_sum, diff_sq = (ln_tmp[:, i, :] for i in range(4))
                nc.vector.tensor_tensor(mean_sum, stats[:, :, 1], stats[:, :, 4], ALU.add).then_inc(ln_moments, 1)
                nc.vector.tensor_tensor(mean_diff, stats[:, :, 1], stats[:, :, 4], ALU.subtract).then_inc(ln_moments, 1)
                nc.vector.tensor_tensor(moment_sum, stats[:, :, 2], stats[:, :, 5], ALU.add).then_inc(ln_moments, 1)
                dve.wait_ge(ln_moments, 6 * (g + done) + 3)
                nc.vector.tensor_scalar(mean[:], mean_sum, 0.5, None, ALU.mult).then_inc(ln_moments, 1)
                nc.vector.scalar_tensor_tensor(out=diff_sq, in0=mean_diff, scalar=0.25, in1=mean_diff,
                                               op0=ALU.mult, op1=ALU.mult).then_inc(ln_moments, 1)
                nc.vector.tensor_scalar(moment_sum, moment_sum, 1.0 / D, EPS, ALU.mult, ALU.add).then_inc(ln_moments, 1)
                dve.wait_ge(ln_moments, 6 * (g + done) + 6)
                nc.vector.tensor_tensor(var_eps[:], moment_sum, diff_sq, ALU.add).then_inc(ln_var, 1)

            def layernorm_apply(g, first=False, done=0):
                dve.wait_ge(ln_rstd, g + done + 1)
                if done:
                    nc.vector.tensor_copy(qscale[:], rstd[:]).then_inc(ln_scale, 1)
                else:
                    nc.vector.tensor_tensor(qscale[:], rstd[:], mask_cols[:, bass.ds(GB * g, GB)], ALU.mult).then_inc(ln_scale, 1)
                dve.wait_ge(ln_scale, g + done + 1)
                if not first:
                    dve.wait_ge(xqt_done, g + done)
                for b in range(GB):
                    nc.vector.tensor_scalar(xq[:, b, :], xs[:, GB * g + b, :], mean[:, b:b + 1], qscale[:, b:b + 1],
                                            ALU.subtract, ALU.mult).then_inc(xq_ready, 1)

            def mask_k(g, gp, first=False):
                dve.wait_ge(k_done, g + 1)
                dve.wait_ge(ctx_loaded[gp], 32 * ((g - gp) // 2 + 1))
                if not first:
                    dve.wait_ge(k_split, 4 * g)
                nc.vector.tensor_tensor(k32[:], prep[:], kmask[gp][:], ALU.mult).then_inc(k_masked, 1)

            def take_max(g, j):
                b, u = divmod(j, UNITS)
                dve.wait_ge(smax_done, 4 * UNITS * g + j + 1)
                dst = negmax[:].rearrange("p h i b -> p i h b")[:, 2 * u:2 * u + 2, :, b]
                nc.vector.tensor_reduce(dst, smax[j % 2][:], AX.X, ALU.max, negate=True).then_inc(max_taken, 1)

            def split_shift(g, first=False):
                dve.wait_ge(max_taken, 4 * UNITS * (g + 1))
                if not first:
                    dve.wait_ge(shift_turned, g)
                src = negmax[:].rearrange("p h i b -> p h (i b)")
                nc.vector.tensor_copy(shift[:, :, 0, :], src).then_inc(shift_split, 1)
                dve.wait_ge(shift_split, 4 * g + 1)
                nc.vector.tensor_tensor(shift_rest[:], src, shift[:, :, 0, :], ALU.subtract).then_inc(shift_split, 1)
                dve.wait_ge(shift_split, 4 * g + 2)
                nc.vector.tensor_copy(shift[:, :, 1, :], shift_rest[:]).then_inc(shift_split, 1)
                dve.wait_ge(shift_split, 4 * g + 3)
                nc.vector.tensor_tensor(shift[:, :, 2, :], shift_rest[:], shift[:, :, 1, :], ALU.subtract).then_inc(shift_split, 1)

            def normalise(n, first=False):
                dve.wait_ge(attn_done, n + 1 + CREDIT)
                nc.vector.reciprocal(denom[:], attn_ps[:, :, HD]).then_inc(denom_done, 1)
                dve.wait_ge(denom_done, n + 1)
                if not first:
                    dve.wait_ge(yt_done, n + CREDIT)
                nc.vector.tensor_tensor(y[:], attn_ps[:, :, 0:HD],
                                        denom[:].rearrange("p (h o) -> p h o", o=1).to_broadcast([P, HEADS, HD]),
                                        ALU.mult).then_inc(y_ready, 1)

            def residual(n):
                dve.wait_ge(proj_done, n + 1 + CREDIT)
                nc.vector.tensor_tensor(xs[:, n, :], xs[:, n, :], tail[:, 0:D], ALU.add).then_inc(resid_done, 1)

            dve.wait_ge(x_loaded, 32)
            for g in range(2):
                layernorm_stats(g)
                mask_k(g, g, g == 0)
                layernorm_apply(g, g == 0)
            for j in range(4 * UNITS):
                take_max(0, j)
            split_shift(0, True)

            def group(g, gp, next_group, second_next, start=False):
                j = 0
                for b in range(GB):
                    n = GB * g + b
                    normalise(n, start and b == 0)
                    if next_group:
                        for _ in range(S1_SPREAD[b]):
                            take_max(g + 1, j)
                            j += 1
                        if b == 2:
                            split_shift(g + 1)
                    residual(n)
                    if b == 0 and second_next:
                        layernorm_stats(g + 2)
                        mask_k(g + 2, gp)
                        layernorm_apply(g + 2)

            with dve.Fori(0, GROUPS // 2 - 1) as it:
                for gp in range(2):
                    group(2 * it + gp, gp, True, True)
            group(GROUPS - 2, 0, True, False)
            group(GROUPS - 1, 1, False, False)
            assert steps[0] == 10

            nc.vector.tensor_copy(iota8[:], iota_i[:]).then_inc(router_steps, 1)
            with dve.Fori(0, GROUPS) as g:
                dve.wait_ge(resid_done, BATCH + CREDIT)
                layernorm_stats(g, GROUPS)
                layernorm_apply(g, False, GROUPS)
                count = [0]

                def did(ins, wait=True):
                    count[0] += 1
                    ins.then_inc(router_steps, 1)
                    if wait:
                        dve.wait_ge(router_steps, ROUTER_STEPS * g + count[0] + 1)

                def wide(t):
                    return t[:].rearrange("p (b o) -> p b o", o=1).to_broadcast([P, GB, EXPERTS])

                ids = iota8[:].rearrange("p (o e) -> p o e", o=1).to_broadcast([P, GB, EXPERTS])
                dve.wait_ge(logits_done, g + 1)
                did(nc.vector.tensor_copy(logits[:], tail[:, 0:GB * EXPERTS].rearrange("p (b e) -> p b e", b=GB)))
                for k, src in enumerate((logits, masked)):
                    did(nc.vector.tensor_reduce(top[k][:], src[:], AX.X, ALU.max))
                    if k:
                        did(nc.vector.tensor_tensor(gap[:], top[1][:], top[0][:], ALU.subtract))
                    did(nc.vector.tensor_tensor(tmp8[:], src[:], wide(top[k]), ALU.is_equal))
                    did(nc.vector.scalar_tensor_tensor(out=tmp8[:], in0=tmp8[:], scalar=-float(EXPERTS), in1=ids,
                                                       op0=ALU.mult, op1=ALU.add))
                    did(nc.vector.tensor_reduce(index[:], tmp8[:], AX.X, ALU.min))
                    did(nc.vector.scalar_tensor_tensor(out=chosen[k][:], in0=ids, scalar=-float(EXPERTS), in1=wide(index),
                                                       op0=ALU.add, op1=ALU.is_equal))
                    if not k:
                        did(nc.vector.scalar_tensor_tensor(out=masked[:], in0=chosen[0][:], scalar=-3.0e38, in1=logits[:],
                                                           op0=ALU.mult, op1=ALU.add))
                dve.wait_ge(ratio_done, g + 1)
                did(nc.vector.tensor_scalar(index[:], ratio[:], 1.0, None, ALU.add))
                did(nc.vector.reciprocal(share[0][:], index[:]))
                did(nc.vector.tensor_tensor(share[1][:], share[0][:], ratio[:], ALU.mult))
                did(nc.vector.tensor_tensor(gate[:], chosen[0][:], wide(share[0]), ALU.mult))
                did(nc.vector.tensor_tensor(tmp8[:], chosen[1][:], wide(share[1]), ALU.mult))
                did(nc.vector.tensor_tensor(gate[:], gate[:], tmp8[:], ALU.add))
                assert count[0] == ROUTER_STEPS, count[0]
                dve.wait_ge(bias_done, g + 1)
                for b in range(GB):
                    nc.vector.tensor_tensor(xs[:, GB * g + b, :], xs[:, GB * g + b, :], tail[:, b * D:(b + 1) * D],
                                            ALU.add).then_inc(expert_added, 1)
                for e in range(EXPERTS):
                    dve.wait_ge(expert_done, EXPERTS * g + e + 1)
                    dve.wait_ge(expert_added, (EXPERTS + 1) * GB * g + GB * (e + 1))
                    for b in range(GB):
                        nc.vector.scalar_tensor_tensor(out=xs[:, GB * g + b, :], in0=expert_ps[e % 2][:, b, :],
                                                       scalar=gate[:, b, e:e + 1], in1=xs[:, GB * g + b, :],
                                                       op0=ALU.mult, op1=ALU.add).then_inc(expert_added, 1)


def kernel(x, ctx_1024, mask_BxS2_bf1, L0_xattn_Wq, L0_xattn_Wkv, L0_xattn_Wc, L0_ffn_router_w, L0_ffn_w1, L0_ffn_b1,
           L0_ffn_w2, L0_ffn_b2):
    import numpy as np
    import concourse.bacc as bacc
    from concourse import mybir as mb
    from concourse.bass_utils import run_bass_kernel_spmd

    def lay(a):
        return np.ascontiguousarray(a)

    def pair_columns(w_t):
        return w_t.reshape(D, PAIRS, 2, HD).transpose(0, 2, 3, 1).reshape(D, D)

    x, ctx = np.asarray(x), np.asarray(ctx_1024)
    mask = np.asarray(mask_BxS2_bf1).view(np.uint8)
    wkv_t = np.asarray(L0_xattn_Wkv).T
    arrays = {
        "x": lay(x.transpose(1, 0, 2)),
        "ctx_t": lay(ctx.transpose(2, 0, 1).reshape(D, BATCH * SEQ)),
        "mask": lay(mask.reshape(GROUPS, GT)),
        "mask_t": lay(mask.T),
        "wq_t": lay(pair_columns(np.asarray(L0_xattn_Wq).T)),
        "wkv_t": lay(np.concatenate([pair_columns(wkv_t[:, :D]), wkv_t[:, D:]], axis=1)),
        "wc_t": lay(np.asarray(L0_xattn_Wc).T),
        "router_t": lay(np.asarray(L0_ffn_router_w).T),
        "w1_t": lay(np.asarray(L0_ffn_w1).transpose(2, 0, 1)),
        "b1_t": lay(np.asarray(L0_ffn_b1).reshape(EXPERTS, FC, P).transpose(2, 0, 1)),
        "w2_t": lay(np.asarray(L0_ffn_w2).reshape(EXPERTS, D, FC, P).transpose(3, 0, 2, 1)),
        "b2": lay(np.asarray(L0_ffn_b2)),
    }
    nc = bacc.Bacc("TRN2", target_bir_lowering=False, num_devices=1)
    args = [nc.dram_tensor(f"{name}_dram", a.shape, mb.dt.from_np(a.dtype), kind="ExternalInput").ap()
            for name, a in arrays.items()]
    out = nc.dram_tensor("out_dram", (SEQ, BATCH, D), mb.dt.float32, kind="ExternalOutput").ap()
    xattn_ffn(nc, *args, out)
    r = run_bass_kernel_spmd(nc, [{f"{name}_dram": a for name, a in arrays.items()}], core_ids=[0])
    return r.results[0]["out_dram"].transpose(1, 0, 2)
```

```python
from contextlib import ExitStack

import concourse.bass as bass
from concourse import mybir

F32 = mybir.dt.float32
BF16 = mybir.dt.bfloat16
U8 = mybir.dt.uint8
I32 = mybir.dt.int32
U32 = mybir.dt.uint32
ALU = mybir.AluOpType
ACT = mybir.ActivationFunctionType
AX = mybir.AxisListType

P = 128
BATCH, SEQ, D = 32, 128, 128
HEADS = 16
HD = D // HEADS
PAIRS = HEADS // 2
GB = 4
GROUPS = BATCH // GB
GT = GB * SEQ
GH = GB * HEADS
EPS = 1e-5
EXPERTS, FF = 8, 512
FC = FF // P
HALF = P // 2
SLOT = 2 * HD
SIDE_ROW = 6 * SLOT
SHIFT_ROW = SIDE_ROW + 3
ROWS = SIDE_ROW + 6
Q_PARTS = (0, 0, 1, 1, 0, 2)
K_PARTS = (0, 1, 0, 1, 2, 0)
UNITS = HEADS // 4
UW = 4 * SEQ
GAP_STEP = 9
PICKED_STEP = 14
ROUTER_STEPS = 40
DUMMY_STEP = 7
PADS_STEP = 10
TABLE_STEPS = 31
CREDIT = 1
RING = 3
LOOPED = 6
SHIFT_COLS = 6
TOKENS = BATCH * SEQ
TOPK = 2
REGION = TOKENS + P
ROW = D + 2
TILES = TOKENS * TOPK // P + EXPERTS - 1
TABLE = TILES + 5
SCAN_STEPS = 5
TRING = 4
DROPPED = 2 * TOKENS + 1
HEADROOM = 32


def bf16_parts(value):
    import numpy as np
    rest, parts = np.float32(value), []
    for _ in range(3):
        bits = np.array(rest, np.float32).view(np.uint32)
        top = np.array((int(bits) & 0xFFFF0000), np.uint32).view(np.float32)
        parts.append(float(top))
        rest = np.float32(rest - top)
    return parts


def xattn_ffn(nc, x, ctx_t, mask, mask_t, wq_t, wkv_t, wc_t, router_t, w1_t, b1, w2_t, b2, out):
    stack = ExitStack()
    with stack:
        def sb(name, shape, dt=F32):
            return stack.enter_context(nc.sbuf_tensor(name, shape, dt))

        def ps(name, shape, dt=F32):
            return stack.enter_context(nc.psum_tensor(name, shape, dt))

        def sem(name):
            return stack.enter_context(nc.semaphore(name))

        xs = sb("xs", [P, BATCH, D])
        mask_rows8 = sb("mask_rows8", [GROUPS, GT], U8)
        mask_rows = sb("mask_rows", [GROUPS, GT], BF16)
        mask_cols8 = sb("mask_cols8", [P, BATCH], U8)
        mask_cols = sb("mask_cols", [P, BATCH])
        wq_sb = sb("wq_sb", [P, D])
        wkv_sb = sb("wkv_sb", [P, 2 * D])
        wc_sb = sb("wc_sb", [P, D])
        ident = sb("ident", [P, P])
        ident_b = sb("ident_b", [P, P], BF16)
        ctx_sb = [sb(f"ctx{i}", [P, GT]) for i in range(RING)]
        kmask = [sb(f"kmask{i}", [P, GT], BF16) for i in range(RING)]
        stats = sb("stats", [P, GB, 6])
        mean = sb("mean", [P, GB])
        ln_tmp = sb("ln_tmp", [P, 4, GB])
        var_eps = sb("var_eps", [P, GB])
        minus_half = sb("minus_half", [P, GB])
        zero = sb("zero", [P, 1])
        rstd = sb("rstd", [P, GB])
        qscale = sb("qscale", [P, GB])
        xq = sb("xq", [P, GB, D])
        xq_t = sb("xq_t", [P, GT])
        q32 = sb("q32", [P, GT])
        k32 = sb("k32", [P, GT])
        qpart = [sb(f"qpart{i}", [P, GT], BF16) for i in range(3)]
        kpart = [sb(f"kpart{i}", [P, GT], BF16) for i in range(3)]
        qrest = sb("qrest", [P, GT])
        krest = sb("krest", [P, GT])
        stacks = sb("stacks", [P, 3 * RING * PAIRS * GT // 2])
        QW, KW = PAIRS * GT, PAIRS * GT // 2
        qstack = [stacks[:, i * QW:(i + 1) * QW].bitcast(BF16).rearrange("p (i h t) -> p i h t", i=PAIRS, h=2)
                  for i in range(RING)]
        kstack = [stacks[:, RING * QW + i * KW:RING * QW + (i + 1) * KW].bitcast(BF16)
                  .rearrange("p (i t) -> p i t", i=PAIRS) for i in range(RING)]
        negmax = sb("negmax", [P, PAIRS, 2])
        shift = [sb(f"shift{i}", [P, SHIFT_COLS, HEADS], BF16) for i in range(2)]
        shift_rest = sb("shift_rest", [P, HEADS])
        shift_t = [sb(f"shift_t{i}", [3 * HEADS, SEQ], BF16) for i in range(2)]
        probs = [sb(f"probs{i}", [P, HEADS * SEQ]) for i in range(2)]
        key_terms, query_terms = (t[0:GROUPS, 0:3 * GT].bitcast(BF16).rearrange("g (s t) -> g s t", s=6) for t in probs)
        values = [sb(f"values{i}", [P, GB, HEADS, HEADROOM]) for i in range(RING)]
        denom = sb("denom", [P, HEADS])
        attn_t = sb("attn_t", [P, HEADS // 4, SEQ])
        y = sb("y", [P, HEADS, HD])
        y_t = sb("y_t", [P, SEQ])

        router_sb = sb("router_sb", [P, EXPERTS])
        w1_sb = sb("w1_sb", [P, EXPERTS, FF])
        w2_sb = sb("w2_sb", [P, EXPERTS, FC, D])
        wait_taker = sb("wait_taker", [P, 1])
        iota_i = sb("iota_i", [P, EXPERTS], I32)
        place_i = sb("place_i", [P, TOPK, BATCH], I32)
        first_row_i = sb("first_row_i", [P, EXPERTS], I32)
        lane_i = sb("lane_i", [P, 1], I32)
        tile_lim_i = sb("tile_lim_i", [1, TOKENS // P], I32)
        tile_no_i = sb("tile_no_i", [1, TABLE], I32)
        before = sb("before", [P, P], BF16)
        ones_b = sb("ones_b", [P, P], BF16)

        def carve(region):
            at = [0]

            def take(words):
                at[0] += words
                assert at[0] <= region.shape[1], (at[0], region.shape)
                return region[:, at[0] - words:at[0]]
            return take

        take = carve(stacks[:])
        b1_sb = take(EXPERTS * FF)
        b2_sb = take(EXPERTS * D)
        rows_all = take(BATCH * TOPK * ROW)
        rows_out = rows_all.rearrange("p (b k r) -> p b k r", b=BATCH, k=TOPK)
        found = [rows_all[:, k * BATCH * D:(k + 1) * BATCH * D].rearrange("p (b d) -> p b d", b=BATCH)
                 for k in range(TOPK)]
        by_batch = [take(BATCH * EXPERTS).rearrange("p (b e) -> p b e", b=BATCH) for _ in range(7)]
        logits, masked, tmp8, totals_a, totals_b, *chosen = by_batch
        picked = take(BATCH * EXPERTS // 2).bitcast(BF16).rearrange("p (b e) -> p b e", b=BATCH)
        stats2 = take(BATCH * 6).rearrange("p (b s) -> p b s", b=BATCH)
        top = [take(BATCH) for _ in range(2)]
        index, gap, ratio, mean2, var2, rstd2, mean_sum2, mean_diff2, moment_sum2, diff_sq2 = (take(BATCH) for _ in range(10))
        share = [take(BATCH) for _ in range(2)]
        row_f = take(TOPK * BATCH)
        row_i = take(TOPK * BATCH).bitcast(U32).rearrange("p (k b) -> p k b", k=TOPK)
        xg = [take(ROW) for _ in range(TRING)]
        y_out = [take(D) for _ in range(TRING)]

        take = carve(values[2][:].rearrange("p b h c -> p (b h c)"))
        iota8, first_row, last_row, row_pad = (take(EXPERTS) for _ in range(4))
        pad_at = take(EXPERTS).bitcast(U32)
        lane = take(1)
        pad_row = take(ROW)
        lone = carve(values[1][0:1].rearrange("p b h c -> p (b h c)"))
        tile_lim = lone(TOKENS // P)
        tile_no, expert_f = lone(TABLE), lone(TABLE)
        tile_f = [lone(TABLE) for _ in range(3)]
        expert_of, start_of = (lone(TABLE).bitcast(I32) for _ in range(2))
        used, tiles = lone(EXPERTS), lone(EXPERTS)
        ends = [lone(EXPERTS) for _ in range(2)]
        lone = carve(values[0][0:1].rearrange("p b h c -> p (b h c)"))
        over = lone(EXPERTS * (TOKENS // P)).rearrange("p (e j) -> p e j", e=EXPERTS)
        passed, passed2 = (lone(TABLE * EXPERTS).rearrange("p (t e) -> p t e", t=TABLE) for _ in range(2))
        normed_t = [xq_t[:], ctx_sb[2][:]]
        flat = [probs[i][:] for i in range(2)]
        xg_t = [flat[i][:, 0:P] for i in range(2)]
        biased = [flat[i][:, P:P + FF] for i in range(2)]
        hidden = [flat[i][:, P + FF:P + 2 * FF] for i in range(2)]
        y_sum = [flat[i][:, P + 2 * FF:2 * P + 2 * FF] for i in range(2)]

        smax = [ps(f"smax{i}", [P, 2, 2, SEQ]) for i in range(2)]
        sexp = [ps(f"sexp{i}", [P, 4, 2, SEQ]) for i in range(2)]
        prep = ps("prep", [P, GT])
        tail = ps("tail", [P, GT])
        shift_ps = prep[:].bitcast(BF16)
        attn_ps = tail[:].rearrange("p (h q) -> p h q", q=SEQ)
        heads_ps = tail[:].rearrange("p (h c) -> p h c", c=HEADROOM)

        key_terms_d = nc.dram_tensor("key_terms_d", [GROUPS, 6, GT], BF16, kind="Internal").ap()
        query_terms_d = nc.dram_tensor("query_terms_d", [GROUPS, 6, GT], BF16, kind="Internal").ap()
        mask_d = nc.dram_tensor("mask_d", [GROUPS, GT], BF16, kind="Internal").ap()

        dispatch_d = nc.dram_tensor("dispatch_d", [EXPERTS * REGION + P, ROW], F32, kind="Internal").ap()
        result_d = nc.dram_tensor("result_d", [TOPK * TOKENS, D], F32, kind="Internal").ap()

        x_loaded = sem("x_loaded")
        weights_loaded = sem("weights_loaded")
        masks_loaded = sem("masks_loaded")
        terms_stored = sem("terms_stored")
        ctx_loaded = [sem(f"ctx_loaded{i}") for i in range(RING)]
        stacks_loaded = [sem(f"stacks_loaded{i}") for i in range(RING)]
        shift_loaded = [sem(f"shift_loaded{i}") for i in range(2)]
        ident_zero = sem("ident_zero")
        before_set = sem("before_set")
        ident_made = sem("ident_made")
        cleared = sem("cleared")
        shift_cleared = sem("shift_cleared")
        values_set = sem("values_set")
        mask_prep = sem("mask_prep")
        ln_stats = sem("ln_stats")
        ln_moments = sem("ln_moments")
        ln_var = sem("ln_var")
        ln_rstd = sem("ln_rstd")
        ln_scale = sem("ln_scale")
        xq_ready = sem("xq_ready")
        xqt_done = sem("xqt_done")
        xqt_copied = sem("xqt_copied")
        q_done = sem("q_done")
        q_copied = sem("q_copied")
        k_done = sem("k_done")
        k_masked = sem("k_masked")
        v_done = sem("v_done")
        v_copied = sem("v_copied")
        q_split = sem("q_split")
        k_split = sem("k_split")
        smax_done = sem("smax_done")
        max_taken = sem("max_taken")
        shift_split = sem("shift_split")
        shift_turned = sem("shift_turned")
        shift_copied = sem("shift_copied")
        sexp_done = sem("sexp_done")
        exp_done = sem("exp_done")
        attn_done = sem("attn_done")
        attn_copied = sem("attn_copied")
        heads_done = sem("heads_done")
        denom_done = sem("denom_done")
        y_ready = sem("y_ready")
        yt_done = sem("yt_done")
        yt_copied = sem("yt_copied")
        proj_done = sem("proj_done")
        resid_done = sem("resid_done")
        out_stored = sem("out_stored")
        router_steps = sem("router_steps")
        ratio_done = sem("ratio_done")
        logits_done = sem("logits_done")
        rows_normed = sem("rows_normed")
        rows_copied = sem("rows_copied")
        rows_sent = sem("rows_sent")
        ranks_done = sem("ranks_done")
        pads_sent = sem("pads_sent")
        wait_taken = sem("wait_taken")
        idle_rows_stored = sem("idle_rows_stored")
        table_steps = sem("table_steps")
        bias_loaded = sem("bias_loaded")
        xg_loaded = [sem(f"xg_loaded{i}") for i in range(TRING)]
        xg_turned = sem("xg_turned")
        xg_copied = sem("xg_copied")
        up_done = sem("up_done")
        bias_added = sem("bias_added")
        hidden_turned = sem("hidden_turned")
        gelu_done = sem("gelu_done")
        down_done = sem("down_done")
        y_summed = sem("y_summed")
        y_gated = sem("y_gated")
        y_sent = [sem(f"y_sent{i}") for i in range(TRING)]
        found_loaded = [sem(f"found_loaded{i}") for i in range(GROUPS)]
        found_added = sem("found_added")
        ffn_loaded = sem("ffn_loaded")

        STACK_DMAS = len(K_PARTS) + 2 * len(Q_PARTS) + 2
        neg = bf16_parts(-1e9)

        def stacks_ready(eng, g, gp):
            eng.wait_ge(stacks_loaded[gp], 16 * STACK_DMAS * ((g - gp) // RING + 1))

        def ctx_ready(eng, g, gp):
            eng.wait_ge(ctx_loaded[gp], 32 * ((g - gp) // RING + 1))

        up_ps = [smax[i][:].rearrange("p i h q -> p (i h q)") for i in range(2)]
        turned_ps = [sexp[0][:].rearrange("p i h q -> p (i h q)")[:, i * FF:(i + 1) * FF] for i in range(2)]
        down_ps = [sexp[1][:].rearrange("p i h q -> p (i h q)")[:, i * FF:i * FF + D] for i in range(2)]
        xg_ps = [prep[:, 0:P], tail[:, 0:P]]
        before_ps = smax[0][:].rearrange("p i h q -> p (i h q)")[:, 0:BATCH * EXPERTS]
        count_ps = smax[0][:].rearrange("p i h q -> p (i h q)")[:, BATCH * EXPERTS:2 * BATCH * EXPERTS]
        normed_ps = [prep[:], up_ps[1]]

        def ring_count(t, r):
            return 16 * ((t - r) // TRING + 1)

        block = stack.enter_context(nc.Block())

        @block.sync
        def _(sp):
            sp.dma_start(mask_rows8[:], mask).then_inc(masks_loaded, 16)
            sp.dma_start(mask_cols8[:], mask_t).then_inc(masks_loaded, 16)

            sp.dma_start(xs[:, 0:GB, :], x[:, 0:GB, :]).then_inc(x_loaded, 16)
            sp.dma_start(xs[:, GB:, :], x[:, GB:, :]).then_inc(x_loaded, 16)
            sp.dma_start(wq_sb[:], wq_t).then_inc(weights_loaded, 16)
            sp.dma_start(wkv_sb[:], wkv_t).then_inc(weights_loaded, 16)
            sp.dma_start(wc_sb[:], wc_t).then_inc(weights_loaded, 16)
            for dst, src in ((router_sb, router_t), (w1_sb, w1_t), (w2_sb, w2_t)):
                sp.dma_start(dst[:], src).then_inc(ffn_loaded, 16)
            sp.wait_ge(mask_prep, 10)
            sp.dma_start(key_terms_d, key_terms).then_inc(terms_stored, 16)
            sp.dma_start(query_terms_d, query_terms).then_inc(terms_stored, 16)
            sp.dma_start(mask_d, mask_rows[:]).then_inc(terms_stored, 16)
            sp.wait_ge(terms_stored, 48)

            def load_ctx(g, gp):
                sp.dma_start(ctx_sb[gp][:], ctx_t[:, bass.ds(g * GT, GT)]).then_inc(ctx_loaded[gp], 16)
                sp.dma_start(kmask[gp][:], mask_d[bass.ds(g, 1), :].to_broadcast([P, GT])).then_inc(ctx_loaded[gp], 16)

            def stack_part(gp, part, step, g):
                sp.wait_ge(k_split if step == "k" else q_split, 4 * g + (1, 3, 4)[part])
                for slot in range(len(K_PARTS)):
                    if step == "k" and K_PARTS[slot] == part:
                        sp.dma_start(kstack[gp][SLOT * slot:SLOT * (slot + 1)], kpart[part][:]).then_inc(stacks_loaded[gp], 16)
                    if step == "q" and Q_PARTS[slot] == part:
                        for hp in range(2):
                            row = SLOT * slot + HD * hp
                            sp.dma_start(qstack[gp][row:row + HD, :, hp, :],
                                         qpart[part][HALF * hp:HALF * (hp + 1), :]).then_inc(stacks_loaded[gp], 16)

            def load_terms(g, gp):
                for tile, terms, copies in ((kstack[gp], key_terms_d, PAIRS), (qstack[gp], query_terms_d, HEADS)):
                    src = terms[bass.ds(g, 1), :, :].rearrange("g s t -> (g s) t").rearrange("s (o t) -> s o t", o=1)
                    sp.dma_start(tile[SIDE_ROW:ROWS], src.to_broadcast([6, copies, GT])).then_inc(stacks_loaded[gp], 16)

            def load_shift(n, g, gp, b):
                sp.wait_ge(shift_copied, n + 1)
                rows = qstack[gp][SHIFT_ROW:ROWS].rearrange("s i h t -> s (i h) t")
                sp.dma_start(rows[:, :, b * SEQ:(b + 1) * SEQ], shift_t[b % 2][:]).then_inc(shift_loaded[b % 2], 16)

            load_ctx(0, 0)
            load_ctx(1, 1)
            sp.wait_ge(cleared, RING)
            for g in range(2):
                load_terms(g, g)
                for side in "kq":
                    for part in range(3):
                        stack_part(g, part, side, g)
            for b in range(GB - 1):
                load_shift(b, 0, 0, b)

            def group(g, gp, next_group, second_next):
                ahead, two_ahead = (gp + 1) % RING, (gp + 2) % RING
                if second_next:
                    load_ctx(g + 2, two_ahead)
                    sp.wait_ge(sexp_done, 8 * g + 2)
                    load_terms(g + 2, two_ahead)
                load_shift(GB * g + 3, g, gp, 3)
                if second_next:
                    for part in range(3):
                        stack_part(two_ahead, part, "k", g + 2)
                if next_group:
                    load_shift(GB * g + 4, g + 1, ahead, 0)
                if second_next:
                    stack_part(two_ahead, 0, "q", g + 2)
                if next_group:
                    load_shift(GB * g + 5, g + 1, ahead, 1)
                if second_next:
                    for part in (1, 2):
                        stack_part(two_ahead, part, "q", g + 2)
                if next_group:
                    load_shift(GB * g + 6, g + 1, ahead, 2)

            with sp.Fori(0, LOOPED // RING) as it:
                for gp in range(RING):
                    group(RING * it + gp, gp, True, True)
            group(GROUPS - 2, 0, True, False)
            group(GROUPS - 1, 1, False, False)
            sp.wait_ge(attn_done, BATCH + CREDIT)
            sp.dma_start(b1_sb, b1.to_broadcast([P, EXPERTS * FF])).then_inc(bias_loaded, 16)
            sp.dma_start(b2_sb, b2.to_broadcast([P, EXPERTS * D])).then_inc(bias_loaded, 16)
            sp.wait_ge(table_steps, DUMMY_STEP)
            sp.dma_start(dispatch_d[EXPERTS * REGION:, :], pad_row).then_inc(idle_rows_stored, 16)
            sp.wait_ge(rows_sent, 16 * TOPK * BATCH)
            sp.wait_ge(pads_sent, 16 * EXPERTS)
            sp.wait_ge(idle_rows_stored, 16)
            sp.wait_ge(table_steps, TABLE_STEPS)

            def load_tile(t, r, reuse):
                if reuse:
                    sp.wait_ge(y_sent[r], ring_count(t - TRING, r))
                at = sp.value_load(start_of[0:1, bass.ds(t, 1)], min_val=0, max_val=EXPERTS * REGION)
                sp.dma_start(xg[r], dispatch_d[bass.ds(at, P), :]).then_inc(xg_loaded[r], 16)

            for t in range(TRING):
                load_tile(t, t, False)
            with sp.Fori(0, (TILES + 1) // TRING - 1) as it:
                for r in range(TRING):
                    load_tile(TRING * it + TRING + r, r, True)
            for r in range(TRING):
                sp.wait_ge(y_sent[r], 16 * ((TILES - 1 - r) // TRING + 1))
            found_d = result_d.rearrange("(k p b) d -> k p b d", k=TOPK, b=BATCH)
            for g in range(GROUPS):
                part = slice(GB * g, GB * (g + 1))
                for k in range(TOPK):
                    sp.dma_start(found[k][:, part, :], found_d[k, :, part, :]).then_inc(found_loaded[g], 16)
            for g in range(GROUPS):
                part = slice(GB * g, GB * (g + 1))
                sp.wait_ge(found_added, 2 * (g + 1))
                sp.dma_start(out[:, part, :], xs[:, part, :]).then_inc(out_stored, 16)
            sp.wait_ge(out_stored, 16 * GROUPS)

        @block.gpsimd
        def _(pool):
            nc.gpsimd.memset(ident[:], 0.0).then_inc(ident_zero, 1)
            nc.gpsimd.memset(ident_b[:], 0.0).then_inc(ident_zero, 1)
            pool.wait_ge(ident_zero, 2)
            for m in (ident, ident_b):
                nc.gpsimd.affine_select(out=m[:], in_=m[:], compare_op=ALU.not_equal, fill=1.0, base=0,
                                        pattern=[[-1, P]], channel_multiplier=1).then_inc(ident_made, 1)
            nc.gpsimd.iota(iota_i[:], [[1, EXPERTS]], base=EXPERTS, channel_multiplier=0).then_inc(ident_made, 1)
            nc.gpsimd.iota(place_i[:], [[TOKENS, TOPK], [1, BATCH]], base=0, channel_multiplier=BATCH).then_inc(ident_made, 1)
            nc.gpsimd.iota(first_row_i[:], [[REGION, EXPERTS]], base=0, channel_multiplier=0).then_inc(ident_made, 1)
            nc.gpsimd.iota(lane_i[:], [[1, 1]], base=0, channel_multiplier=1).then_inc(ident_made, 1)
            nc.gpsimd.iota(tile_lim_i[:], [[P, TOKENS // P]], base=0, channel_multiplier=0).then_inc(ident_made, 1)
            nc.gpsimd.iota(tile_no_i[:], [[1, TABLE]], base=0, channel_multiplier=0).then_inc(ident_made, 1)
            nc.gpsimd.memset(ones_b[:], 1.0).then_inc(ident_made, 1)
            nc.gpsimd.memset(before[:], 1.0).then_inc(before_set, 1)
            pool.wait_ge(before_set, 1)
            nc.gpsimd.affine_select(out=before[:], in_=before[:], compare_op=ALU.is_gt, fill=0.0, base=0,
                                    pattern=[[1, P]], channel_multiplier=-1).then_inc(ident_made, 1)
            nc.gpsimd.memset(minus_half[:], -0.5).then_inc(ident_made, 1)
            nc.gpsimd.memset(zero[:], 0.0).then_inc(ident_made, 1)
            pool.wait_ge(ident_made, 12)
            for i in range(RING):
                nc.gpsimd.memset(values[i][:], 1.0).then_inc(values_set, 1)

            no_shift = zero[:].to_broadcast([P, GT])

            def split(g, src, parts, rest, src_ready, step):
                pool.wait_ge(src_ready, g + 1)
                nc.gpsimd.tensor_tensor(parts[0][:], src[:], no_shift, ALU.add).then_inc(step, 1)
                pool.wait_ge(step, 4 * g + 1)
                nc.gpsimd.tensor_tensor(rest[:], src[:], parts[0][:], ALU.subtract).then_inc(step, 1)
                pool.wait_ge(step, 4 * g + 2)
                nc.gpsimd.tensor_tensor(parts[1][:], rest[:], no_shift, ALU.add).then_inc(step, 1)
                pool.wait_ge(step, 4 * g + 3)
                nc.gpsimd.tensor_tensor(parts[2][:], rest[:], parts[1][:], ALU.subtract).then_inc(step, 1)

            def splits(g, gp, reuse):
                pool.wait_ge(ln_var, g + 1)
                nc.gpsimd.tensor_tensor(rstd[:], var_eps[:], minus_half[:], ALU.pow).then_inc(ln_rstd, 1)
                if reuse:
                    stacks_ready(pool, g - 1, (gp - 1) % RING)
                split(g, k32, kpart, krest, k_masked, k_split)
                split(g, q32, qpart, qrest, q_copied, q_split)

            splits(0, 0, False)
            splits(1, 1, True)
            with pool.Fori(0, LOOPED // RING) as it:
                for gp in range(RING):
                    splits(RING * it + gp + 2, (gp + 2) % RING, True)
            pool.wait_ge(ln_var, GROUPS + 1)
            nc.gpsimd.tensor_tensor(rstd2, var2, minus_half[:, 0:1].to_broadcast([P, BATCH]), ALU.pow).then_inc(ln_rstd, 1)
            pool.wait_ge(router_steps, ROUTER_STEPS)
            pool.wait_ge(rows_copied, GROUPS)
            for b in range(BATCH):
                for k in range(TOPK):
                    nc.gpsimd.indirect_dma_start(
                        out=dispatch_d, out_offset=bass.IndirectOffsetOnAxis(ap=row_i[:, k, b:b + 1], axis=0),
                        in_=rows_out[:, b, k, :], in_offset=None).then_inc(rows_sent, 16)
            pool.wait_ge(table_steps, PADS_STEP)
            pool.wait_ge(rows_sent, 16 * TOPK * BATCH)
            for e in range(EXPERTS):
                nc.gpsimd.indirect_dma_start(
                    out=dispatch_d, out_offset=bass.IndirectOffsetOnAxis(ap=pad_at[:, e:e + 1], axis=0),
                    in_=pad_row, in_offset=None).then_inc(pads_sent, 16)

            def store_tile(t, r, first=False):
                if not first:
                    pool.wait_ge(wait_taken, t)
                pool.wait_ge(y_gated, t + 1)
                nc.gpsimd.tensor_tensor(wait_taker[:], zero[:], zero[:], ALU.add).then_inc(wait_taken, 1)
                nc.gpsimd.indirect_dma_start(
                    out=result_d, out_offset=bass.IndirectOffsetOnAxis(ap=xg[r][:, D + 1:D + 2].bitcast(U32), axis=0),
                    in_=y_out[r], in_offset=None, bounds_check=TOPK * TOKENS - 1,
                    oob_is_err=False).then_inc(y_sent[r], 16)

            store_tile(0, 0, True)
            with pool.Fori(0, (TILES - 3) // TRING) as it:
                for j in range(TRING):
                    store_tile(TRING * it + j + 1, (j + 1) % TRING)
            for t in range(TILES - 2, TILES):
                store_tile(t, t % TRING)

        @block.scalar
        def _(act):
            def copy_xqt(g, first=False):
                act.wait_ge(xqt_done, g + 1)
                if not first:
                    act.wait_ge(q_done, g)
                nc.scalar.activation(xq_t[:], prep[:], ACT.Copy).then_inc(xqt_copied, 1)

            def copy_q(g, first=False):
                act.wait_ge(q_done, g + 1)
                if not first:
                    act.wait_ge(q_split, 4 * g)
                nc.scalar.activation(q32[:], prep[:], ACT.Copy).then_inc(q_copied, 1)

            def copy_v(g, gp, first=False):
                act.wait_ge(v_done, g + 1)
                if not first:
                    act.wait_ge(attn_done, 4 * (g - 1))
                nc.scalar.activation(values[gp][:, :, :, 0:HD],
                                     prep[:].rearrange("p (b h d) -> p b h d", b=GB, d=HD),
                                     ACT.Copy).then_inc(v_copied, 1)

            def copy_shift(n, b, first=False):
                act.wait_ge(shift_turned, n + 1)
                if not first:
                    act.wait_ge(shift_loaded[b % 2], 16 * ((n - b % 2) // 2))
                nc.scalar.activation(shift_t[b % 2][:], shift_ps[0:3 * HEADS, 0:SEQ], ACT.Copy).then_inc(shift_copied, 1)

            def copy_attn(n):
                act.wait_ge(attn_done, n + 1 + CREDIT)
                act.wait_ge(heads_done, n + CREDIT)
                nc.scalar.activation(attn_t[:], attn_ps, ACT.Copy).then_inc(attn_copied, 1)

            def exp(n, np_, u, free):
                act.wait_ge(sexp_done, 2 * n + u + 1)
                if free:
                    act.wait_ge(attn_done, n - 1 + CREDIT)
                w = HEADS * SEQ // 2
                nc.scalar.activation(probs[np_][:, u * w:(u + 1) * w],
                                     sexp[u][:].rearrange("p i h q -> p (i h q)"), ACT.Exp).then_inc(exp_done, 1)

            def copy_yt(n, first):
                act.wait_ge(yt_done, n + 1 + CREDIT)
                if not first:
                    act.wait_ge(proj_done, n + CREDIT)
                nc.scalar.activation(y_t[:], tail[:, 0:SEQ], ACT.Copy).then_inc(yt_copied, 1)

            act.wait_ge(values_set, RING)
            for g in range(2):
                copy_xqt(g, g == 0)
                copy_q(g, g == 0)
            copy_v(0, 0, True)
            for b in range(GB - 1):
                copy_shift(b, b, b < 2)
            for u in range(2):
                exp(0, 0, u, False)

            def group(g, gp, next_group, second_next):
                for b in range(GB):
                    n = GB * g + b
                    more = b < GB - 1 or next_group
                    copy_attn(n)
                    if more:
                        exp(n + 1, (b + 1) % 2, 0, True)
                    if b == 0 or next_group:
                        copy_shift(n + 3, (b + 3) % GB)
                    copy_yt(n, False)
                    if more:
                        exp(n + 1, (b + 1) % 2, 1, True)
                    if b == 1 and second_next:
                        copy_xqt(g + 2)
                    if b == 1 and second_next:
                        copy_q(g + 2)
                    if b == 2 and next_group:
                        copy_v(g + 1, (gp + 1) % RING)

            with act.Fori(0, LOOPED // RING) as it:
                for gp in range(RING):
                    group(RING * it + gp, gp, True, True)
            group(GROUPS - 2, 0, True, False)
            group(GROUPS - 1, 1, False, False)

            for g in range(GROUPS):
                part = slice(GB * g, GB * (g + 1))
                act.wait_ge(xqt_done, GROUPS + g + 1)
                if g >= 2:
                    act.wait_ge(logits_done, g - 1)
                nc.scalar.activation(normed_t[g % 2], normed_ps[g % 2], ACT.Copy).then_inc(xqt_copied, 1)
                nc.scalar.activation(rows_out[:, part, 1, 0:D], rows_out[:, part, 0, 0:D], ACT.Copy).then_inc(rows_copied, 1)
            act.wait_ge(router_steps, GAP_STEP)
            nc.scalar.activation(ratio, gap, ACT.Exp).then_inc(ratio_done, 1)

            def copy_xg(t, i):
                act.wait_ge(xg_turned, t + 1)
                nc.scalar.activation(xg_t[i], xg_ps[i], ACT.Copy).then_inc(xg_copied, 1)

            def gelu(t, i):
                act.wait_ge(hidden_turned, t + 1)
                nc.scalar.activation(hidden[i], turned_ps[i], ACT.Gelu).then_inc(gelu_done, 1)

            def gate_y(t, i, r):
                act.wait_ge(y_summed, t + 1)
                nc.scalar.activation(y_out[r], y_sum[i], ACT.Copy, scale=xg[r][:, D:D + 1]).then_inc(y_gated, 1)

            def tile_step(t, j):
                gate_y(t - 1, (j + 1) % 2, (j - 1) % TRING)
                gelu(t, j % 2)
                copy_xg(t + 1, (j + 1) % 2)

            copy_xg(0, 0)
            gelu(0, 0)
            copy_xg(1, 1)
            with act.Fori(0, (TILES - 3) // TRING) as it:
                for j in range(TRING):
                    tile_step(TRING * it + j + 1, j + 1)
            for t in range(TILES - 2, TILES):
                tile_step(t, t)
            gate_y(TILES - 1, (TILES - 1) % 2, (TILES - 1) % TRING)

        @block.tensor
        def _(pe):
            def turn_xq(g):
                pe.wait_ge(xq_ready, GB * (g + 1))
                for b in range(GB):
                    last = nc.tensor.transpose(prep[:, b * SEQ:(b + 1) * SEQ], xq[:, b, :], ident[:])
                last.then_inc(xqt_done, 1)

            def project_q(g):
                pe.wait_ge(xqt_copied, g + 1)
                nc.tensor.matmul(prep[:], wq_sb[:], xq_t[:], start=True, stop=True).then_inc(q_done, 1)

            def project_k(g, gp):
                ctx_ready(pe, g, gp)
                nc.tensor.matmul(prep[:], wkv_sb[:, 0:D], ctx_sb[gp][:], start=True, stop=True).then_inc(k_done, 1)

            def project_v(g, gp):
                for b in range(GB):
                    last = nc.tensor.matmul(prep[:, b * D:(b + 1) * D], ctx_sb[gp][:, b * SEQ:(b + 1) * SEQ],
                                            wkv_sb[:, D:2 * D], start=True, stop=True)
                last.then_inc(v_done, 1)

            def turn_shift(n, b):
                pe.wait_ge(shift_split, 4 * (n + 1))
                nc.tensor.transpose(shift_ps[0:SHIFT_COLS * HEADS, 0:SEQ], shift[b % 2][:].rearrange("p s c -> p (s c)"),
                                    ident_b[:]).then_inc(shift_turned, 1)

            def scores_for_max(g, gp, j, free):
                b, u = divmod(j, UNITS)
                if free or j >= 2:
                    pe.wait_ge(max_taken, 4 * UNITS * g + j - 1)
                ks = slice(b * SEQ, (b + 1) * SEQ)
                for i in range(2):
                    for hp in range(2):
                        last = nc.tensor.matmul(smax[j % 2][:, i, hp, :], qstack[gp][0:ROWS, 2 * u + i, hp, ks],
                                                kstack[gp][0:ROWS, 2 * u + i, ks], start=True, stop=True)
                last.then_inc(smax_done, 1)

            def scores_for_exp(n, b, gp, u, free):
                if free:
                    pe.wait_ge(exp_done, 2 * n + u - 1)
                ks = slice(b * SEQ, (b + 1) * SEQ)
                for i in range(4):
                    last = nc.tensor.matmul(sexp[u][:, i, :, :], kstack[gp][0:ROWS, 4 * u + i, ks],
                                            qstack[gp][0:ROWS, 4 * u + i, :, ks], start=True, stop=True)
                last.then_inc(sexp_done, 1)

            def attend(n, b, gp, first):
                pe.wait_ge(exp_done, 2 * n + 2)
                if not first:
                    pe.wait_ge(resid_done, n + CREDIT)
                for h in range(HEADS):
                    rows = slice(HEADROOM * (h % 4), HEADROOM * (h % 4 + 1))
                    last = nc.tensor.matmul(attn_ps[rows, h // 4, :], values[gp][:, b, h, :],
                                            probs[b % 2][:, h * SEQ:(h + 1) * SEQ], start=True, stop=True)
                last.then_inc(attn_done, 1)

            def turn_heads(n):
                pe.wait_ge(attn_copied, n + 1)
                for c in range(HEADS // 4):
                    last = nc.tensor.transpose(tail[:, c * P:(c + 1) * P], attn_t[:, c, :], ident[:])
                last.then_inc(heads_done, 1)

            def turn_y(n):
                pe.wait_ge(y_ready, n + 1)
                nc.tensor.transpose(tail[:, 0:SEQ], y[:].rearrange("p h d -> p (h d)"), ident[:]).then_inc(yt_done, 1)

            def project_y(n):
                pe.wait_ge(yt_copied, n + 1)
                nc.tensor.matmul(tail[:, 0:D], y_t[:], wc_sb[:], start=True, stop=True).then_inc(proj_done, 1)

            for begun in (attn_done, heads_done, yt_done, proj_done):
                pe.sem_inc(begun, CREDIT)
            pe.wait_ge(weights_loaded, 48)
            pe.wait_ge(ident_made, 2)
            for g in range(2):
                if g:
                    pe.wait_ge(q_copied, g)
                project_k(g, g)
                pe.wait_ge(k_masked, g + 1)
                turn_xq(g)
                project_q(g)
            pe.wait_ge(q_copied, 2)
            project_v(0, 0)
            stacks_ready(pe, 0, 0)
            for b in range(GB):
                for u in range(UNITS):
                    scores_for_max(0, 0, UNITS * b + u, False)
                if b:
                    pe.wait_ge(v_copied, 1) if b == 1 else pe.wait_ge(shift_copied, b - 1)
                    turn_shift(b - 1, b - 1)
            pe.wait_ge(shift_loaded[0], 16)
            for u in range(2):
                scores_for_exp(0, 0, 0, u, False)

            def group(g, gp, next_group, second_next):
                ahead, two_ahead = (gp + 1) % RING, (gp + 2) % RING
                for b in range(GB):
                    n = GB * g + b
                    more = b < GB - 1 or next_group
                    ngp, nb = (gp, b + 1) if b < GB - 1 else (ahead, 0)
                    attend(n, b, gp, False)
                    if more:
                        pe.wait_ge(shift_loaded[nb % 2], 16 * ((n + 1 - nb % 2) // 2 + 1))
                        scores_for_exp(n + 1, nb, ngp, 0, True)
                    if next_group:
                        if b == 0:
                            stacks_ready(pe, g + 1, ahead)
                        for u in range(2):
                            scores_for_max(g + 1, ahead, UNITS * b + u, True)
                    turn_heads(n)
                    if b == 3 and next_group:
                        pe.wait_ge(v_copied, g + 2)
                    elif b == 1 and second_next:
                        pe.wait_ge(k_masked, g + 3)
                    elif b == 2 and second_next:
                        pe.wait_ge(q_copied, g + 3)
                    elif b == 0 or next_group:
                        pe.wait_ge(shift_copied, n + 3)
                    if b == 0 or next_group:
                        turn_shift(n + 3, (b + 3) % GB)
                    if more:
                        scores_for_exp(n + 1, nb, ngp, 1, True)
                    if next_group:
                        scores_for_max(g + 1, ahead, UNITS * b + 2, True)
                    turn_y(n)
                    if b < 2 and second_next or b == 2 and next_group:
                        pe.wait_ge(shift_copied, n + 4)
                    if b == 0 and second_next:
                        project_k(g + 2, two_ahead)
                    if b == 1 and second_next:
                        turn_xq(g + 2)
                    if b == 2 and next_group:
                        project_v(g + 1, ahead)
                    if next_group:
                        scores_for_max(g + 1, ahead, UNITS * b + 3, True)
                    project_y(n)
                    if b == 1 and second_next:
                        project_q(g + 2)

            with pe.Fori(0, LOOPED // RING) as it:
                for gp in range(RING):
                    group(RING * it + gp, gp, True, True)
            group(GROUPS - 2, 0, True, False)
            group(GROUPS - 1, 1, False, False)

            pe.wait_ge(ffn_loaded, 3 * 16)
            def project_router(g):
                pe.wait_ge(xqt_copied, GROUPS + g + 1)
                for b in range(GB):
                    n = GB * g + b
                    last = nc.tensor.matmul(tail[:, n * EXPERTS:(n + 1) * EXPERTS], normed_t[g % 2][:, b * SEQ:(b + 1) * SEQ],
                                            router_sb[:], start=True, stop=True)
                last.then_inc(logits_done, 1)

            for g in range(GROUPS):
                pe.wait_ge(rows_normed, GB * (g + 1))
                if g >= 2:
                    pe.wait_ge(xqt_copied, GROUPS + g - 1)
                for b in range(GB):
                    last = nc.tensor.transpose(normed_ps[g % 2][:, b * SEQ:(b + 1) * SEQ], rows_out[:, GB * g + b, 0, 0:D],
                                               ident[:])
                last.then_inc(xqt_done, 1)
                if g:
                    project_router(g - 1)
            project_router(GROUPS - 1)
            pe.wait_ge(router_steps, PICKED_STEP)
            all_picked = picked.rearrange("p b e -> p (b e)")
            nc.tensor.matmul(before_ps, before[:], all_picked, start=True, stop=True)
            nc.tensor.matmul(count_ps, ones_b[:], all_picked, start=True, stop=True).then_inc(ranks_done, 1)

            def turn_tile(t, i, r, first=False):
                pe.wait_ge(xg_loaded[r], ring_count(t, r))
                if not first:
                    pe.wait_ge(xg_copied, t)
                nc.tensor.transpose(xg_ps[i], xg[r][:, 0:D], ident[:]).then_inc(xg_turned, 1)

            def up(t, i, e):
                pe.wait_ge(xg_copied, t + 1)
                nc.tensor.matmul(up_ps[i], xg_t[i], w1_sb[:].rearrange("p e f -> p (e f)")[:, bass.ds(e * FF, FF)],
                                 start=True, stop=True).then_inc(up_done, 1)

            def turn_hidden(t, i):
                pe.wait_ge(bias_added, t + 1)
                for c in range(FC):
                    last = nc.tensor.transpose(turned_ps[i][:, c * P:(c + 1) * P], biased[i][:, c * P:(c + 1) * P], ident[:])
                last.then_inc(hidden_turned, 1)

            def down(t, i, e):
                pe.wait_ge(gelu_done, t + 1)
                for c in range(FC):
                    last = nc.tensor.matmul(down_ps[i], hidden[i][:, c * P:(c + 1) * P],
                                            w2_sb[:].rearrange("p e c d -> p (e c d)")[:, bass.ds(e * FF + c * D, D)],
                                            start=(c == 0), stop=(c == FC - 1))
                last.then_inc(down_done, 1)

            def expert_reg(t):
                return pe.value_load(expert_of[0:1, bass.ds(t, 1)], min_val=0, max_val=EXPERTS - 1)

            def tile_step(t, j):
                up(t, j % 2, expert_reg(t))
                down(t - 1, (j + 1) % 2, expert_reg(t - 1))
                turn_hidden(t, j % 2)
                turn_tile(t + 1, (j + 1) % 2, (j + 1) % TRING)

            pe.wait_ge(table_steps, TABLE_STEPS)
            turn_tile(0, 0, 0, True)
            up(0, 0, expert_reg(0))
            turn_hidden(0, 0)
            turn_tile(1, 1, 1, True)
            with pe.Fori(0, (TILES - 3) // TRING) as it:
                for j in range(TRING):
                    tile_step(TRING * it + j + 1, j + 1)
            for t in range(TILES - 2, TILES):
                tile_step(t, t)
            down(TILES - 1, (TILES - 1) % 2, expert_reg(TILES - 1))

        @block.vector
        def _(dve):
            steps = [0]

            def step(ins):
                steps[0] += 1
                ins.then_inc(mask_prep, 1)

            dve.sem_inc(resid_done, CREDIT)
            dve.wait_ge(masks_loaded, 32)
            step(nc.vector.tensor_copy(mask_rows[:], mask_rows8[:]))
            step(nc.vector.tensor_scalar(mask_cols[:], mask_cols8[:], float(HD) ** -0.5, None, ALU.mult))
            step(nc.vector.memset(key_terms[:, 3:6, :], 1.0))
            step(nc.vector.memset(query_terms[:, 3:6, :], 0.0))
            dve.wait_ge(mask_prep, 4)
            for i in range(2):
                nc.vector.memset(shift[i][:], 0.0).then_inc(shift_cleared, 1)
            for i in range(RING):
                nc.vector.memset(stacks[:, i * QW:(i + 1) * QW].bitcast(U32), 0).then_inc(cleared, 1)
            for s in range(3):
                step(nc.vector.tensor_scalar(key_terms[:, s, :], mask_rows[:], -neg[s], neg[s], ALU.mult, ALU.add))
                step(nc.vector.tensor_copy(query_terms[:, s, :], mask_rows[:]))

            def layernorm_stats(g, done=0):
                for b in range(GB):
                    nc.vector.bn_stats(stats[:, b, :], xs[:, GB * g + b, :]).then_inc(ln_stats, 1)
                dve.wait_ge(ln_stats, GB * (g + done + 1))
                mean_sum, mean_diff, moment_sum, diff_sq = (ln_tmp[:, i, :] for i in range(4))
                nc.vector.tensor_tensor(mean_sum, stats[:, :, 1], stats[:, :, 4], ALU.add).then_inc(ln_moments, 1)
                nc.vector.tensor_tensor(mean_diff, stats[:, :, 1], stats[:, :, 4], ALU.subtract).then_inc(ln_moments, 1)
                nc.vector.tensor_tensor(moment_sum, stats[:, :, 2], stats[:, :, 5], ALU.add).then_inc(ln_moments, 1)
                dve.wait_ge(ln_moments, 6 * (g + done) + 3)
                nc.vector.tensor_scalar(mean[:], mean_sum, 0.5, None, ALU.mult).then_inc(ln_moments, 1)
                nc.vector.scalar_tensor_tensor(out=diff_sq, in0=mean_diff, scalar=0.25, in1=mean_diff,
                                               op0=ALU.mult, op1=ALU.mult).then_inc(ln_moments, 1)
                nc.vector.tensor_scalar(moment_sum, moment_sum, 1.0 / D, EPS, ALU.mult, ALU.add).then_inc(ln_moments, 1)
                dve.wait_ge(ln_moments, 6 * (g + done) + 6)
                nc.vector.tensor_tensor(var_eps[:], moment_sum, diff_sq, ALU.add).then_inc(ln_var, 1)

            def layernorm_apply(g, first=False, done=0):
                dve.wait_ge(ln_rstd, g + done + 1)
                if done:
                    nc.vector.tensor_copy(qscale[:], rstd[:]).then_inc(ln_scale, 1)
                else:
                    nc.vector.tensor_tensor(qscale[:], rstd[:], mask_cols[:, bass.ds(GB * g, GB)], ALU.mult).then_inc(ln_scale, 1)
                dve.wait_ge(ln_scale, g + done + 1)
                if not first:
                    dve.wait_ge(xqt_done, g + done)
                for b in range(GB):
                    nc.vector.tensor_scalar(xq[:, b, :], xs[:, GB * g + b, :], mean[:, b:b + 1], qscale[:, b:b + 1],
                                            ALU.subtract, ALU.mult).then_inc(xq_ready, 1)

            def mask_k(g, gp, first=False):
                dve.wait_ge(k_done, g + 1)
                ctx_ready(dve, g, gp)
                if not first:
                    dve.wait_ge(k_split, 4 * g)
                nc.vector.tensor_tensor(k32[:], prep[:], kmask[gp][:], ALU.mult).then_inc(k_masked, 1)

            def take_max(g, j):
                b, u = divmod(j, UNITS)
                dve.wait_ge(smax_done, 4 * UNITS * g + j + 1)
                dst = negmax[:, 2 * u:2 * u + 2, :]
                nc.vector.tensor_reduce(dst, smax[j % 2][:], AX.X, ALU.max, negate=True).then_inc(max_taken, 1)

            def split_shift(n, b, first=False):
                dve.wait_ge(max_taken, UNITS * (n + 1))
                if not first:
                    dve.wait_ge(shift_turned, n - 1)
                src = negmax[:].rearrange("p i h -> p (i h)")
                part = shift[b % 2]
                nc.vector.tensor_copy(part[:, 0, :], src).then_inc(shift_split, 1)
                dve.wait_ge(shift_split, 4 * n + 1)
                nc.vector.tensor_tensor(shift_rest[:], src, part[:, 0, :], ALU.subtract).then_inc(shift_split, 1)
                dve.wait_ge(shift_split, 4 * n + 2)
                nc.vector.tensor_copy(part[:, 1, :], shift_rest[:]).then_inc(shift_split, 1)
                dve.wait_ge(shift_split, 4 * n + 3)
                nc.vector.tensor_tensor(part[:, 2, :], shift_rest[:], part[:, 1, :], ALU.subtract).then_inc(shift_split, 1)

            def normalise(n, first=False):
                dve.wait_ge(heads_done, n + 1 + CREDIT)
                nc.vector.reciprocal(denom[:], heads_ps[:, :, HD]).then_inc(denom_done, 1)
                dve.wait_ge(denom_done, n + 1)
                if not first:
                    dve.wait_ge(yt_done, n + CREDIT)
                nc.vector.tensor_tensor(y[:], heads_ps[:, :, 0:HD],
                                        denom[:].rearrange("p (h o) -> p h o", o=1).to_broadcast([P, HEADS, HD]),
                                        ALU.mult).then_inc(y_ready, 1)

            def residual(n):
                dve.wait_ge(proj_done, n + 1 + CREDIT)
                nc.vector.tensor_tensor(xs[:, n, :], xs[:, n, :], tail[:, 0:D], ALU.add).then_inc(resid_done, 1)

            dve.wait_ge(x_loaded, 32)
            for g in range(2):
                layernorm_stats(g)
                mask_k(g, g, g == 0)
                layernorm_apply(g, g == 0)
            dve.wait_ge(shift_cleared, 2)
            for b in range(GB):
                for u in range(UNITS):
                    take_max(0, UNITS * b + u)
                split_shift(b, b, b < 2)

            def group(g, gp, next_group, second_next):
                for b in range(GB):
                    n = GB * g + b
                    if next_group:
                        for u in range(2):
                            take_max(g + 1, UNITS * b + u)
                    normalise(n)
                    if next_group:
                        for u in range(2, UNITS):
                            take_max(g + 1, UNITS * b + u)
                        split_shift(n + GB, b)
                    residual(n)
                    if b == 0 and second_next:
                        layernorm_stats(g + 2)
                        mask_k(g + 2, (gp + 2) % RING)
                        layernorm_apply(g + 2)

            with dve.Fori(0, LOOPED // RING) as it:
                for gp in range(RING):
                    group(RING * it + gp, gp, True, True)
            group(GROUPS - 2, 0, True, False)
            group(GROUPS - 1, 1, False, False)
            assert steps[0] == 10

            dve.wait_ge(resid_done, BATCH + CREDIT)
            table = [0]

            def link(ins):
                table[0] += 1
                ins.then_inc(table_steps, 1)
                dve.wait_ge(table_steps, table[0])

            routed = [0]

            def did(ins):
                routed[0] += 1
                ins.then_inc(router_steps, 1)
                dve.wait_ge(router_steps, routed[0])

            for n in range(BATCH):
                nc.vector.bn_stats(stats2[:, n, :], xs[:, n, :]).then_inc(ln_stats, 1)
            for dst, src in ((first_row, first_row_i), (iota8, iota_i), (lane, lane_i), (tile_lim, tile_lim_i), (tile_no, tile_no_i)):
                link(nc.vector.tensor_copy(dst, src[:]))
            link(nc.vector.memset(pad_row, 0.0))
            link(nc.vector.memset(pad_row[:, D + 1:D + 2].bitcast(I32), DROPPED))
            assert table[0] == DUMMY_STEP
            dve.wait_ge(ln_stats, GB * GROUPS + BATCH)
            nc.vector.tensor_tensor(mean_sum2, stats2[:, :, 1], stats2[:, :, 4], ALU.add).then_inc(ln_moments, 1)
            nc.vector.tensor_tensor(mean_diff2, stats2[:, :, 1], stats2[:, :, 4], ALU.subtract).then_inc(ln_moments, 1)
            nc.vector.tensor_tensor(moment_sum2, stats2[:, :, 2], stats2[:, :, 5], ALU.add).then_inc(ln_moments, 1)
            dve.wait_ge(ln_moments, 6 * GROUPS + 3)
            nc.vector.tensor_scalar(mean2, mean_sum2, 0.5, None, ALU.mult).then_inc(ln_moments, 1)
            nc.vector.scalar_tensor_tensor(out=diff_sq2, in0=mean_diff2, scalar=0.25, in1=mean_diff2,
                                           op0=ALU.mult, op1=ALU.mult).then_inc(ln_moments, 1)
            nc.vector.tensor_scalar(moment_sum2, moment_sum2, 1.0 / D, EPS, ALU.mult, ALU.add).then_inc(ln_moments, 1)
            dve.wait_ge(ln_moments, 6 * GROUPS + 6)
            nc.vector.tensor_tensor(var2, moment_sum2, diff_sq2, ALU.add).then_inc(ln_var, 1)
            dve.wait_ge(ln_rstd, GROUPS + 1)
            for n in range(BATCH):
                nc.vector.tensor_scalar(rows_out[:, n, 0, 0:D], xs[:, n, :], mean2[:, n:n + 1], rstd2[:, n:n + 1],
                                        ALU.subtract, ALU.mult).then_inc(rows_normed, 1)

            def wide(t):
                return t.rearrange("p (b o) -> p b o", o=1).to_broadcast([P, BATCH, EXPERTS])

            ids = iota8.rearrange("p (o e) -> p o e", o=1).to_broadcast([P, BATCH, EXPERTS])
            dve.wait_ge(logits_done, GROUPS)
            did(nc.vector.tensor_copy(logits, tail[:, 0:BATCH * EXPERTS].rearrange("p (b e) -> p b e", b=BATCH)))
            for k, src in enumerate((logits, masked)):
                did(nc.vector.tensor_reduce(top[k], src, AX.X, ALU.max))
                if k:
                    did(nc.vector.tensor_tensor(gap, top[1], top[0], ALU.subtract))
                    assert routed[0] == GAP_STEP, routed[0]
                did(nc.vector.tensor_tensor(tmp8, src, wide(top[k]), ALU.is_equal))
                did(nc.vector.scalar_tensor_tensor(out=tmp8, in0=tmp8, scalar=-float(EXPERTS), in1=ids,
                                                   op0=ALU.mult, op1=ALU.add))
                did(nc.vector.tensor_reduce(index, tmp8, AX.X, ALU.min))
                did(nc.vector.scalar_tensor_tensor(out=chosen[k], in0=ids, scalar=-float(EXPERTS), in1=wide(index),
                                                   op0=ALU.add, op1=ALU.is_equal))
                if not k:
                    did(nc.vector.scalar_tensor_tensor(out=masked, in0=chosen[0], scalar=-3.0e38, in1=logits,
                                                       op0=ALU.mult, op1=ALU.add))
            did(nc.vector.tensor_tensor(picked, chosen[0], chosen[1], ALU.add))
            assert routed[0] == PICKED_STEP, routed[0]
            dve.wait_ge(ratio_done, 1)
            did(nc.vector.tensor_scalar(index, ratio, 1.0, None, ALU.add))
            did(nc.vector.reciprocal(share[0], index))
            did(nc.vector.tensor_tensor(share[1], share[0], ratio, ALU.mult))
            for k in range(TOPK):
                did(nc.vector.tensor_copy(rows_out[:, :, k, D], share[k]))
                did(nc.vector.tensor_copy(rows_out[:, :, k, D + 1].bitcast(I32), place_i[:, k, :]))
            dve.wait_ge(ranks_done, 1)
            totals = (totals_a, totals_b)
            did(nc.vector.tensor_copy(totals_a, count_ps.rearrange("p (b e) -> p b e", b=BATCH)))
            for n in range(SCAN_STEPS):
                hop, a, b = 1 << n, totals[n % 2], totals[(n + 1) % 2]
                did(nc.vector.tensor_copy(b[:, 0:hop, :], a[:, 0:hop, :]))
                did(nc.vector.tensor_tensor(b[:, hop:, :], a[:, hop:, :], a[:, 0:BATCH - hop, :], ALU.add))
            total, rank = totals[SCAN_STEPS % 2], totals[(SCAN_STEPS + 1) % 2]
            did(nc.vector.tensor_tensor(rank[:, 0, :], before_ps[:, 0:EXPERTS], first_row, ALU.add))
            did(nc.vector.tensor_tensor(rank[:, 1:, :], total[:, 0:BATCH - 1, :],
                                        first_row.rearrange("p (o e) -> p o e", o=1).to_broadcast([P, BATCH - 1, EXPERTS]),
                                        ALU.add))
            did(nc.vector.tensor_tensor(rank[:, 1:, :], rank[:, 1:, :],
                                        before_ps[:, EXPERTS:].rearrange("p (b e) -> p b e", e=EXPERTS), ALU.add))
            for k in range(TOPK):
                did(nc.vector.tensor_tensor(chosen[k], chosen[k], rank, ALU.mult))
                did(nc.vector.tensor_reduce(row_f[:, k * BATCH:(k + 1) * BATCH], chosen[k], AX.X, ALU.add))
            did(nc.vector.tensor_copy(row_i.rearrange("p k b -> p (k b)"), row_f))
            assert routed[0] == ROUTER_STEPS, routed[0]

            link(nc.vector.tensor_tensor(last_row, total[:, BATCH - 1, :], first_row, ALU.add))
            link(nc.vector.tensor_scalar(row_pad, last_row, lane, None, ALU.add))
            link(nc.vector.tensor_copy(pad_at, row_pad))
            assert table[0] == PADS_STEP
            link(nc.vector.tensor_tensor(used, last_row[0:1, :], first_row[0:1, :], ALU.subtract))
            link(nc.vector.tensor_tensor(over, used.rearrange("p (e o) -> p e o", o=1).to_broadcast([1, EXPERTS, TOKENS // P]),
                                         tile_lim.rearrange("p (o j) -> p o j", o=1).to_broadcast([1, EXPERTS, TOKENS // P]),
                                         ALU.is_gt))
            link(nc.vector.tensor_reduce(tiles, over, AX.X, ALU.add))
            link(nc.vector.tensor_copy(ends[0], tiles))
            for n, hop in enumerate((1, 2, 4)):
                a, b = ends[n % 2], ends[(n + 1) % 2]
                link(nc.vector.tensor_copy(b[:, 0:hop], a[:, 0:hop]))
                link(nc.vector.tensor_tensor(b[:, hop:], a[:, hop:], a[:, 0:EXPERTS - hop], ALU.add))
            wide_no = tile_no.rearrange("p (t o) -> p t o", o=1).to_broadcast([1, TABLE, EXPERTS])

            def by_expert(t):
                return t.rearrange("p (o e) -> p o e", o=1).to_broadcast([1, TABLE, EXPERTS])

            link(nc.vector.tensor_tensor(passed, wide_no, by_expert(ends[1]), ALU.is_ge))
            link(nc.vector.tensor_reduce(expert_f, passed, AX.X, ALU.add))
            link(nc.vector.tensor_tensor(passed2, passed, by_expert(tiles), ALU.mult))
            link(nc.vector.tensor_reduce(tile_f[0], passed2, AX.X, ALU.add))
            link(nc.vector.tensor_tensor(tile_f[1], tile_no, tile_f[0], ALU.subtract))
            link(nc.vector.tensor_scalar(tile_f[2], expert_f, float(EXPERTS), float(P), ALU.is_lt, ALU.mult))
            link(nc.vector.tensor_tensor(tile_f[0], tile_f[1], tile_f[2], ALU.mult))
            link(nc.vector.scalar_tensor_tensor(out=tile_f[1], in0=expert_f, scalar=float(REGION), in1=tile_f[0],
                                                op0=ALU.mult, op1=ALU.add))
            link(nc.vector.tensor_copy(start_of, tile_f[1]))
            link(nc.vector.tensor_scalar(tile_f[2], expert_f, float(EXPERTS - 1), None, ALU.min))
            link(nc.vector.tensor_copy(expert_of, tile_f[2]))
            assert table[0] == TABLE_STEPS, table[0]

            def expert_reg(t):
                return dve.value_load(expert_of[0:1, bass.ds(t, 1)], min_val=0, max_val=EXPERTS - 1)

            def add_bias(t, i, e):
                dve.wait_ge(up_done, t + 1)
                nc.vector.tensor_tensor(biased[i], up_ps[i], b1_sb[:, bass.ds(e * FF, FF)], ALU.add).then_inc(bias_added, 1)

            def sum_y(t, i, e):
                dve.wait_ge(down_done, t + 1)
                nc.vector.tensor_tensor(y_sum[i], down_ps[i], b2_sb[:, bass.ds(e * D, D)], ALU.add).then_inc(y_summed, 1)

            def tile_step(t, j):
                add_bias(t, j % 2, expert_reg(t))
                sum_y(t - 1, (j + 1) % 2, expert_reg(t - 1))

            dve.wait_ge(bias_loaded, 32)
            add_bias(0, 0, expert_reg(0))
            with dve.Fori(0, (TILES - 3) // TRING) as it:
                for j in range(TRING):
                    tile_step(TRING * it + j + 1, j + 1)
            for t in range(TILES - 2, TILES):
                tile_step(t, t)
            sum_y(TILES - 1, (TILES - 1) % 2, expert_reg(TILES - 1))
            for g in range(GROUPS):
                part = slice(GB * g, GB * (g + 1))
                dve.wait_ge(found_loaded[g], 32)
                for k in range(TOPK):
                    nc.vector.tensor_tensor(xs[:, part, :], xs[:, part, :], found[k][:, part, :], ALU.add).then_inc(found_added, 1)
                    if not k:
                        dve.wait_ge(found_added, 2 * g + 1)


def kernel(x, ctx_1024, mask_BxS2_bf1, L0_xattn_Wq, L0_xattn_Wkv, L0_xattn_Wc, L0_ffn_router_w, L0_ffn_w1, L0_ffn_b1,
           L0_ffn_w2, L0_ffn_b2):
    import numpy as np
    import concourse.bacc as bacc
    from concourse import mybir as mb
    from concourse.bass_utils import run_bass_kernel_spmd

    def lay(a):
        return np.ascontiguousarray(a)

    def pair_columns(w_t):
        return w_t.reshape(D, PAIRS, 2, HD).transpose(0, 2, 3, 1).reshape(D, D)

    x, ctx = np.asarray(x), np.asarray(ctx_1024)
    mask = np.asarray(mask_BxS2_bf1).view(np.uint8)
    wkv_t = np.asarray(L0_xattn_Wkv).T
    arrays = {
        "x": lay(x.transpose(1, 0, 2)),
        "ctx_t": lay(ctx.transpose(2, 0, 1).reshape(D, BATCH * SEQ)),
        "mask": lay(mask.reshape(GROUPS, GT)),
        "mask_t": lay(mask.T),
        "wq_t": lay(pair_columns(np.asarray(L0_xattn_Wq).T)),
        "wkv_t": lay(np.concatenate([pair_columns(wkv_t[:, :D]), wkv_t[:, D:]], axis=1)),
        "wc_t": lay(np.asarray(L0_xattn_Wc).T),
        "router_t": lay(np.asarray(L0_ffn_router_w).T),
        "w1_t": lay(np.asarray(L0_ffn_w1).transpose(2, 0, 1)),
        "b1": lay(np.asarray(L0_ffn_b1).reshape(1, EXPERTS * FF)),
        "w2_t": lay(np.asarray(L0_ffn_w2).reshape(EXPERTS, D, FC, P).transpose(3, 0, 2, 1)),
        "b2": lay(np.asarray(L0_ffn_b2).reshape(1, EXPERTS * D)),
    }
    nc = bacc.Bacc("TRN2", target_bir_lowering=False, num_devices=1)
    args = [nc.dram_tensor(f"{name}_dram", a.shape, mb.dt.from_np(a.dtype), kind="ExternalInput").ap()
            for name, a in arrays.items()]
    out = nc.dram_tensor("out_dram", (SEQ, BATCH, D), mb.dt.float32, kind="ExternalOutput").ap()
    xattn_ffn(nc, *args, out)
    r = run_bass_kernel_spmd(nc, [{f"{name}_dram": a for name, a in arrays.items()}], core_ids=[0])
    return r.results[0]["out_dram"].transpose(1, 0, 2)
```

```python
from contextlib import ExitStack

import concourse.bass as bass
from concourse import mybir

F32 = mybir.dt.float32
BF16 = mybir.dt.bfloat16
U8 = mybir.dt.uint8
I32 = mybir.dt.int32
U32 = mybir.dt.uint32
ALU = mybir.AluOpType
ACT = mybir.ActivationFunctionType
AX = mybir.AxisListType

P = 128
BATCH, SEQ, D = 32, 128, 128
HEADS = 16
HD = D // HEADS
PAIRS = HEADS // 2
GB = 4
GROUPS = BATCH // GB
GT = GB * SEQ
EPS = 1e-5
EXPERTS, FF = 8, 512
FC = FF // P
HALF = P // 2
SLOT = 2 * HD
SIDE_ROW = 6 * SLOT
SHIFT_ROW = SIDE_ROW + 3
ROWS = SIDE_ROW + 6
Q_PARTS = (0, 0, 1, 1, 0, 2)
K_PARTS = (0, 1, 0, 1, 2, 0)
UNITS = HEADS // 4
UW = 4 * SEQ
GAP_STEP = 9
PICKED_STEP = 14
ROUTER_STEPS = 40
DUMMY_STEP = 7
PADS_STEP = 10
TABLE_STEPS = 31
CREDIT = 1
RING = 3
LOOPED = 6
SHIFT_COLS = 6
TOKENS = BATCH * SEQ
TOPK = 2
REGION = TOKENS + P
ROW = D + 2
TILES = TOKENS * TOPK // P + EXPERTS - 1
TABLE = TILES + 5
SCAN_STEPS = 5
TRING = 8
LOOPED_TILES = (TILES - 2) // TRING * TRING
DROPPED = 2 * TOKENS + 1
HEADROOM = 32


def bf16_parts(value):
    import numpy as np
    rest, parts = np.float32(value), []
    for _ in range(3):
        bits = np.array(rest, np.float32).view(np.uint32)
        top = np.array((int(bits) & 0xFFFF0000), np.uint32).view(np.float32)
        parts.append(float(top))
        rest = np.float32(rest - top)
    return parts


def xattn_ffn(nc, x, ctx_t, mask, mask_t, wq_t, wkv_t, wc_t, router_t, w1_t, b1, w2_t, b2, out):
    stack = ExitStack()
    with stack:
        def sb(name, shape, dt=F32):
            return stack.enter_context(nc.sbuf_tensor(name, shape, dt))

        def ps(name, shape, dt=F32):
            return stack.enter_context(nc.psum_tensor(name, shape, dt))

        def sem(name):
            return stack.enter_context(nc.semaphore(name))

        xs_all = sb("xs_all", [P, 1 + BATCH, D])
        xs = xs_all[:, 1:, :]
        mask_rows8 = sb("mask_rows8", [GROUPS, GT], U8)
        mask_rows = sb("mask_rows", [GROUPS, GT], BF16)
        mask_cols8 = sb("mask_cols8", [P, BATCH], U8)
        mask_cols = sb("mask_cols", [P, BATCH])
        wq_sb = sb("wq_sb", [P, D])
        wkv_sb = sb("wkv_sb", [P, 2 * D])
        wc_sb = sb("wc_sb", [P, D])
        ident = sb("ident", [P, P])
        ident_b = sb("ident_b", [P, P], BF16)
        ctx_sb = [sb(f"ctx{i}", [P, GT]) for i in range(RING)]
        kmask = [sb(f"kmask{i}", [P, GT], BF16) for i in range(RING)]
        stats = sb("stats", [P, BATCH, 6])
        mean, var_eps, rstd, qscale, mean_sum, mean_diff, moment_sum, diff_sq = (
            sb(name, [P, BATCH]) for name in
            ("mean", "var_eps", "rstd", "qscale", "mean_sum", "mean_diff", "moment_sum", "diff_sq"))
        minus_half = sb("minus_half", [P, GB])
        zero = sb("zero", [P, 1])
        xq = sb("xq", [P, GB, D])
        xq_t = sb("xq_t", [P, GT])
        q32 = sb("q32", [P, GT])
        k32 = sb("k32", [P, GT])
        qpart = [sb(f"qpart{i}", [P, GT], BF16) for i in range(3)]
        kpart = [sb(f"kpart{i}", [P, GT], BF16) for i in range(3)]
        qrest = sb("qrest", [P, GT])
        krest = sb("krest", [P, GT])
        stacks = sb("stacks", [P, 3 * RING * PAIRS * GT // 2])
        QW, KW = PAIRS * GT, PAIRS * GT // 2
        LAST = (GROUPS - 1) % RING
        others = [i for i in range(RING) if i != LAST]
        q_at = {i: n * QW for n, i in enumerate(others)}
        k_at = {i: len(others) * QW + n * KW for n, i in enumerate(others)}
        q_at[LAST], k_at[LAST] = len(others) * (QW + KW), RING * QW + len(others) * KW
        qstack = [stacks[:, q_at[i]:q_at[i] + QW].bitcast(BF16).rearrange("p (i h t) -> p i h t", i=PAIRS, h=2)
                  for i in range(RING)]
        kstack = [stacks[:, k_at[i]:k_at[i] + KW].bitcast(BF16).rearrange("p (i t) -> p i t", i=PAIRS) for i in range(RING)]
        negmax = sb("negmax", [P, PAIRS, 2])
        shift = [sb(f"shift{i}", [P, SHIFT_COLS, HEADS], BF16) for i in range(2)]
        shift_rest = sb("shift_rest", [P, HEADS])
        shift_t = [sb(f"shift_t{i}", [3 * HEADS, SEQ], BF16) for i in range(2)]
        probs = [sb(f"probs{i}", [P, HEADS * SEQ]) for i in range(2)]
        key_terms, query_terms = (t[0:GROUPS, 0:3 * GT].bitcast(BF16).rearrange("g (s t) -> g s t", s=6) for t in probs)
        values = [sb(f"values{i}", [P, GB, HEADS, HEADROOM]) for i in range(RING)]
        denom = sb("denom", [P, HEADS])
        attn_t = sb("attn_t", [P, HEADS // 4, SEQ])
        y = sb("y", [P, HEADS, HD])
        y_t = sb("y_t", [P, SEQ])

        router_sb = sb("router_sb", [P, EXPERTS])
        w1_sb = sb("w1_sb", [P, EXPERTS, FF])
        w2_sb = sb("w2_sb", [P, EXPERTS, FC, D])
        wait_taker = sb("wait_taker", [P, 1])
        iota_i = sb("iota_i", [P, EXPERTS], I32)
        place_i = sb("place_i", [P, TOPK, BATCH], I32)
        first_row_i = sb("first_row_i", [P, EXPERTS], I32)
        lane_i = sb("lane_i", [P, 1], I32)
        tile_lim_i = sb("tile_lim_i", [1, TOKENS // P], I32)
        tile_no_i = sb("tile_no_i", [1, TABLE], I32)
        before = sb("before", [P, P], BF16)
        ones_b = sb("ones_b", [P, P], BF16)

        def carve(region):
            at = [0]

            def take(words):
                at[0] += words
                assert at[0] <= region.shape[1], (at[0], region.shape)
                return region[:, at[0] - words:at[0]]
            return take

        take = carve(stacks[:])
        b1_sb = stacks[:, q_at[LAST]:q_at[LAST] + EXPERTS * FF]
        b2_sb = stacks[:, k_at[LAST]:k_at[LAST] + EXPERTS * D]
        rows_all = take(BATCH * TOPK * ROW)
        rows_out = rows_all.rearrange("p (b k r) -> p b k r", b=BATCH, k=TOPK)
        found = [rows_all[:, k * BATCH * D:(k + 1) * BATCH * D].rearrange("p (b d) -> p b d", b=BATCH)
                 for k in range(TOPK)]
        by_batch = [take(BATCH * EXPERTS).rearrange("p (b e) -> p b e", b=BATCH) for _ in range(7)]
        logits, masked, tmp8, totals_a, totals_b, *chosen = by_batch
        picked = take(BATCH * EXPERTS // 2).bitcast(BF16).rearrange("p (b e) -> p b e", b=BATCH)
        top = [take(BATCH) for _ in range(2)]
        index, gap, ratio = (take(BATCH) for _ in range(3))
        share = [take(BATCH) for _ in range(2)]
        row_f = take(TOPK * BATCH)
        row_i = take(TOPK * BATCH).bitcast(U32).rearrange("p (k b) -> p k b", k=TOPK)
        xg = [take(ROW) for _ in range(TRING)]

        take = carve(values[2][:].rearrange("p b h c -> p (b h c)"))
        iota8, first_row, last_row, row_pad = (take(EXPERTS) for _ in range(4))
        pad_at = take(EXPERTS).bitcast(U32)
        lane = take(1)
        pad_row = take(ROW)
        y_out = [take(D) for _ in range(TRING)]
        lone = carve(values[1][0:1].rearrange("p b h c -> p (b h c)"))
        tile_lim = lone(TOKENS // P)
        tile_no, expert_f = lone(TABLE), lone(TABLE)
        tile_f = [lone(TABLE) for _ in range(3)]
        expert_of, start_of = (lone(TABLE).bitcast(I32) for _ in range(2))
        used, tiles = lone(EXPERTS), lone(EXPERTS)
        ends = [lone(EXPERTS) for _ in range(2)]
        lone = carve(values[0][0:1].rearrange("p b h c -> p (b h c)"))
        over = lone(EXPERTS * (TOKENS // P)).rearrange("p (e j) -> p e j", e=EXPERTS)
        passed, passed2 = (lone(TABLE * EXPERTS).rearrange("p (t e) -> p t e", t=TABLE) for _ in range(2))
        normed_t = [xq_t[:], ctx_sb[2][:]]
        flat = [probs[i][:] for i in range(2)]
        xg_t = [flat[i][:, 0:P] for i in range(2)]
        biased = [flat[i][:, P:P + FF] for i in range(2)]
        hidden = [flat[i][:, P + FF:P + 2 * FF] for i in range(2)]
        y_sum = [flat[i][:, P + 2 * FF:2 * P + 2 * FF] for i in range(2)]

        smax = [ps(f"smax{i}", [P, 2, 2, SEQ]) for i in range(2)]
        sexp = [ps(f"sexp{i}", [P, 4, 2, SEQ]) for i in range(2)]
        prep = ps("prep", [P, GT])
        tail = ps("tail", [P, GT])
        shift_ps = prep[:].bitcast(BF16)
        attn_ps = tail[:].rearrange("p (h q) -> p h q", q=SEQ)
        heads_ps = tail[:].rearrange("p (h c) -> p h c", c=HEADROOM)

        key_terms_d = nc.dram_tensor("key_terms_d", [GROUPS, 6, GT], BF16, kind="Internal").ap()
        query_terms_d = nc.dram_tensor("query_terms_d", [GROUPS, 6, GT], BF16, kind="Internal").ap()
        mask_d = nc.dram_tensor("mask_d", [GROUPS, GT], BF16, kind="Internal").ap()

        dispatch_d = nc.dram_tensor("dispatch_d", [EXPERTS * REGION + P, ROW], F32, kind="Internal").ap()
        result_d = nc.dram_tensor("result_d", [TOPK * TOKENS, D], F32, kind="Internal").ap()

        x_loaded = sem("x_loaded")
        x_rest_loaded = sem("x_rest_loaded")
        weights_loaded = sem("weights_loaded")
        masks_loaded = sem("masks_loaded")
        terms_stored = sem("terms_stored")
        ctx_loaded = [sem(f"ctx_loaded{i}") for i in range(RING)]
        stacks_loaded = [sem(f"stacks_loaded{i}") for i in range(RING)]
        shift_loaded = [sem(f"shift_loaded{i}") for i in range(2)]
        ident_zero = sem("ident_zero")
        before_set = sem("before_set")
        ident_made = sem("ident_made")
        cleared = sem("cleared")
        shift_cleared = sem("shift_cleared")
        values_set = sem("values_set")
        mask_prep = sem("mask_prep")
        ln_stats = sem("ln_stats")
        ln_moments = sem("ln_moments")
        ln_var = sem("ln_var")
        ln_rstd = sem("ln_rstd")
        ln_scale = sem("ln_scale")
        xq_ready = sem("xq_ready")
        xqt_done = sem("xqt_done")
        xqt_copied = sem("xqt_copied")
        q_done = sem("q_done")
        q_copied = sem("q_copied")
        k_done = sem("k_done")
        k_masked = sem("k_masked")
        v_done = sem("v_done")
        v_copied = sem("v_copied")
        q_split = sem("q_split")
        k_split = sem("k_split")
        smax_done = sem("smax_done")
        max_taken = sem("max_taken")
        shift_split = sem("shift_split")
        shift_turned = sem("shift_turned")
        shift_copied = sem("shift_copied")
        sexp_done = sem("sexp_done")
        exp_done = sem("exp_done")
        attn_done = sem("attn_done")
        attn_copied = sem("attn_copied")
        heads_done = sem("heads_done")
        denom_done = sem("denom_done")
        y_ready = sem("y_ready")
        yt_done = sem("yt_done")
        yt_copied = sem("yt_copied")
        proj_done = sem("proj_done")
        resid_done = sem("resid_done")
        out_stored = sem("out_stored")
        router_steps = sem("router_steps")
        ratio_done = sem("ratio_done")
        logits_done = sem("logits_done")
        rows_normed = sem("rows_normed")
        rows_copied = sem("rows_copied")
        rows_sent = sem("rows_sent")
        ranks_done = sem("ranks_done")
        pads_sent = sem("pads_sent")
        wait_taken = sem("wait_taken")
        idle_rows_stored = sem("idle_rows_stored")
        table_steps = sem("table_steps")
        bias_loaded = sem("bias_loaded")
        xg_loaded = [sem(f"xg_loaded{i}") for i in range(TRING)]
        xg_turned = sem("xg_turned")
        xg_copied = sem("xg_copied")
        up_done = sem("up_done")
        bias_added = sem("bias_added")
        hidden_turned = sem("hidden_turned")
        gelu_done = sem("gelu_done")
        down_done = sem("down_done")
        y_summed = sem("y_summed")
        y_gated = sem("y_gated")
        y_sent = [sem(f"y_sent{i}") for i in range(TRING)]
        found_loaded = [sem(f"found_loaded{i}") for i in range(GROUPS)]
        found_added = sem("found_added")
        ffn_loaded = sem("ffn_loaded")

        assert EXPERTS == GROUPS
        STACK_DMAS = len(K_PARTS) + 2 * len(Q_PARTS) + 2
        neg = bf16_parts(-1e9)

        def stacks_ready(eng, g, gp):
            eng.wait_ge(stacks_loaded[gp], 16 * STACK_DMAS * ((g - gp) // RING + 1))

        def ctx_ready(eng, g, gp):
            eng.wait_ge(ctx_loaded[gp], 32 * ((g - gp) // RING + 1))

        up_ps = [smax[i][:].rearrange("p i h q -> p (i h q)") for i in range(2)]
        turned_ps = [sexp[0][:].rearrange("p i h q -> p (i h q)")[:, i * FF:(i + 1) * FF] for i in range(2)]
        down_ps = [sexp[1][:].rearrange("p i h q -> p (i h q)")[:, i * FF:i * FF + D] for i in range(2)]
        xg_ps = [prep[:, 0:P], tail[:, 0:P]]
        before_ps = smax[0][:].rearrange("p i h q -> p (i h q)")[:, 0:BATCH * EXPERTS]
        count_ps = smax[0][:].rearrange("p i h q -> p (i h q)")[:, BATCH * EXPERTS:2 * BATCH * EXPERTS]
        normed_ps = [prep[:], up_ps[1]]
        logits_ps = up_ps[0][:, 0:BATCH * EXPERTS]
        TURNED = {1: (0,), 2: (1, 2), 3: (3, 4)}
        LATE = (5, 6, 7)
        EARLY = BATCH - GB
        LN_PARTS = ((0, 2 * GB), (2 * GB, BATCH), (0, EARLY), (EARLY, BATCH))
        APPLIED = {1: range(0, 9), 2: range(9, 18), 3: range(18, EARLY)}

        def ring_count(t, r):
            return 16 * ((t - r) // TRING + 1)

        block = stack.enter_context(nc.Block())

        @block.sync
        def _(sp):
            sp.dma_start(mask_rows8[:], mask).then_inc(masks_loaded, 16)
            sp.dma_start(mask_cols8[:], mask_t).then_inc(masks_loaded, 16)

            sp.dma_start(xs[:, 0:2 * GB, :], x[:, 0:2 * GB, :]).then_inc(x_loaded, 16)
            sp.dma_start(wq_sb[:], wq_t).then_inc(weights_loaded, 16)
            sp.dma_start(wkv_sb[:], wkv_t).then_inc(weights_loaded, 16)
            sp.dma_start(wc_sb[:], wc_t).then_inc(weights_loaded, 16)
            sp.dma_start(router_sb[:], router_t).then_inc(ffn_loaded, 16)
            sp.wait_ge(mask_prep, 10)
            sp.dma_start(key_terms_d, key_terms).then_inc(terms_stored, 16)
            sp.dma_start(query_terms_d, query_terms).then_inc(terms_stored, 16)
            sp.dma_start(mask_d, mask_rows[:]).then_inc(terms_stored, 16)
            sp.wait_ge(terms_stored, 48)

            def load_ctx(g, gp):
                sp.dma_start(ctx_sb[gp][:], ctx_t[:, bass.ds(g * GT, GT)]).then_inc(ctx_loaded[gp], 16)
                sp.dma_start(kmask[gp][:], mask_d[bass.ds(g, 1), :].to_broadcast([P, GT])).then_inc(ctx_loaded[gp], 16)

            def stack_part(gp, part, step, g):
                sp.wait_ge(k_split if step == "k" else q_split, 4 * g + (1, 3, 4)[part])
                for slot in range(len(K_PARTS)):
                    if step == "k" and K_PARTS[slot] == part:
                        sp.dma_start(kstack[gp][SLOT * slot:SLOT * (slot + 1)], kpart[part][:]).then_inc(stacks_loaded[gp], 16)
                    if step == "q" and Q_PARTS[slot] == part:
                        for hp in range(2):
                            row = SLOT * slot + HD * hp
                            sp.dma_start(qstack[gp][row:row + HD, :, hp, :],
                                         qpart[part][HALF * hp:HALF * (hp + 1), :]).then_inc(stacks_loaded[gp], 16)

            def load_terms(g, gp):
                for tile, terms, copies in ((kstack[gp], key_terms_d, PAIRS), (qstack[gp], query_terms_d, HEADS)):
                    src = terms[bass.ds(g, 1), :, :].rearrange("g s t -> (g s) t").rearrange("s (o t) -> s o t", o=1)
                    sp.dma_start(tile[SIDE_ROW:ROWS], src.to_broadcast([6, copies, GT])).then_inc(stacks_loaded[gp], 16)

            def load_shift(n, g, gp, b):
                sp.wait_ge(shift_copied, n + 1)
                rows = qstack[gp][SHIFT_ROW:ROWS].rearrange("s i h t -> s (i h) t")
                sp.dma_start(rows[:, :, b * SEQ:(b + 1) * SEQ], shift_t[b % 2][:]).then_inc(shift_loaded[b % 2], 16)

            load_ctx(0, 0)
            load_ctx(1, 1)
            sp.dma_start(xs[:, 2 * GB:, :], x[:, 2 * GB:, :]).then_inc(x_rest_loaded, 16)
            for g in range(2):
                sp.wait_ge(cleared, g + 1)
                load_terms(g, g)
                for side in "kq":
                    for part in range(3):
                        stack_part(g, part, side, g)
            sp.wait_ge(cleared, RING)
            for b in range(GB - 1):
                load_shift(b, 0, 0, b)

            def group(g, gp, next_group, second_next):
                ahead, two_ahead = (gp + 1) % RING, (gp + 2) % RING
                for weights, src in ((w1_sb, w1_t), (w2_sb, w2_t)):
                    sp.dma_start(weights[:, bass.ds(g, 1)], src[:, bass.ds(g, 1)]).then_inc(ffn_loaded, 16)
                if second_next:
                    load_ctx(g + 2, two_ahead)
                    sp.wait_ge(sexp_done, 8 * g + 2)
                    load_terms(g + 2, two_ahead)
                load_shift(GB * g + 3, g, gp, 3)
                if second_next:
                    for part in range(3):
                        stack_part(two_ahead, part, "k", g + 2)
                if next_group:
                    load_shift(GB * g + 4, g + 1, ahead, 0)
                if second_next:
                    stack_part(two_ahead, 0, "q", g + 2)
                if next_group:
                    load_shift(GB * g + 5, g + 1, ahead, 1)
                if second_next:
                    for part in (1, 2):
                        stack_part(two_ahead, part, "q", g + 2)
                if next_group:
                    load_shift(GB * g + 6, g + 1, ahead, 2)

            with sp.Fori(0, LOOPED // RING) as it:
                for gp in range(RING):
                    group(RING * it + gp, gp, True, True)
            group(GROUPS - 2, 0, True, False)
            group(GROUPS - 1, 1, False, False)
            sp.wait_ge(attn_done, BATCH + CREDIT)
            sp.dma_start(b1_sb, b1.to_broadcast([P, EXPERTS * FF])).then_inc(bias_loaded, 16)
            sp.dma_start(b2_sb, b2.to_broadcast([P, EXPERTS * D])).then_inc(bias_loaded, 16)
            sp.wait_ge(table_steps, DUMMY_STEP)
            sp.dma_start(dispatch_d[EXPERTS * REGION:, :], pad_row).then_inc(idle_rows_stored, 16)
            sp.wait_ge(rows_sent, 16 * TOPK * BATCH)
            sp.wait_ge(pads_sent, 16 * EXPERTS)
            sp.wait_ge(idle_rows_stored, 16)
            sp.wait_ge(table_steps, TABLE_STEPS)

            def load_tile(t, r, reuse):
                if reuse:
                    sp.wait_ge(y_sent[r], ring_count(t - TRING, r))
                at = sp.value_load(start_of[0:1, bass.ds(t, 1)], min_val=0, max_val=EXPERTS * REGION)
                sp.dma_start(xg[r], dispatch_d[bass.ds(at, P), :]).then_inc(xg_loaded[r], 16)

            for t in range(TRING):
                load_tile(t, t, False)
            with sp.Fori(0, (TILES + 1) // TRING - 1) as it:
                for r in range(TRING):
                    load_tile(TRING * it + TRING + r, r, True)
            for r in range(TRING):
                sp.wait_ge(y_sent[r], 16 * ((TILES - 1 - r) // TRING + 1))
            found_d = result_d.rearrange("(k p b) d -> k p b d", k=TOPK, b=BATCH)
            for g in range(GROUPS):
                part = slice(GB * g, GB * (g + 1))
                for k in range(TOPK):
                    sp.dma_start(found[k][:, part, :], found_d[k, :, part, :]).then_inc(found_loaded[g], 16)
            for g in range(GROUPS):
                part = slice(GB * g, GB * (g + 1))
                sp.wait_ge(found_added, 2 * (g + 1))
                sp.dma_start(out[:, part, :], xs[:, part, :]).then_inc(out_stored, 16)
            sp.wait_ge(out_stored, 16 * GROUPS)

        @block.gpsimd
        def _(pool):
            nc.gpsimd.memset(ident[:], 0.0).then_inc(ident_zero, 1)
            nc.gpsimd.memset(ident_b[:], 0.0).then_inc(ident_zero, 1)
            pool.wait_ge(ident_zero, 2)
            for m in (ident, ident_b):
                nc.gpsimd.affine_select(out=m[:], in_=m[:], compare_op=ALU.not_equal, fill=1.0, base=0,
                                        pattern=[[-1, P]], channel_multiplier=1).then_inc(ident_made, 1)
            nc.gpsimd.iota(iota_i[:], [[1, EXPERTS]], base=EXPERTS, channel_multiplier=0).then_inc(ident_made, 1)
            nc.gpsimd.iota(place_i[:], [[TOKENS, TOPK], [1, BATCH]], base=0, channel_multiplier=BATCH).then_inc(ident_made, 1)
            nc.gpsimd.iota(first_row_i[:], [[REGION, EXPERTS]], base=0, channel_multiplier=0).then_inc(ident_made, 1)
            nc.gpsimd.iota(lane_i[:], [[1, 1]], base=0, channel_multiplier=1).then_inc(ident_made, 1)
            nc.gpsimd.iota(tile_lim_i[:], [[P, TOKENS // P]], base=0, channel_multiplier=0).then_inc(ident_made, 1)
            nc.gpsimd.iota(tile_no_i[:], [[1, TABLE]], base=0, channel_multiplier=0).then_inc(ident_made, 1)
            nc.gpsimd.memset(ones_b[:], 1.0).then_inc(ident_made, 1)
            nc.gpsimd.memset(before[:], 1.0).then_inc(before_set, 1)
            pool.wait_ge(before_set, 1)
            nc.gpsimd.affine_select(out=before[:], in_=before[:], compare_op=ALU.is_gt, fill=0.0, base=0,
                                    pattern=[[1, P]], channel_multiplier=-1).then_inc(ident_made, 1)
            nc.gpsimd.memset(minus_half[:], -0.5).then_inc(ident_made, 1)
            nc.gpsimd.memset(zero[:], 0.0).then_inc(ident_made, 1)
            pool.wait_ge(ident_made, 12)
            for i in range(RING):
                nc.gpsimd.memset(values[i][:], 1.0).then_inc(values_set, 1)

            no_shift = zero[:].to_broadcast([P, GT])

            def split(g, src, parts, rest, src_ready, step):
                pool.wait_ge(src_ready, g + 1)
                nc.gpsimd.tensor_tensor(parts[0][:], src[:], no_shift, ALU.add).then_inc(step, 1)
                pool.wait_ge(step, 4 * g + 1)
                nc.gpsimd.tensor_tensor(rest[:], src[:], parts[0][:], ALU.subtract).then_inc(step, 1)
                pool.wait_ge(step, 4 * g + 2)
                nc.gpsimd.tensor_tensor(parts[1][:], rest[:], no_shift, ALU.add).then_inc(step, 1)
                pool.wait_ge(step, 4 * g + 3)
                nc.gpsimd.tensor_tensor(parts[2][:], rest[:], parts[1][:], ALU.subtract).then_inc(step, 1)

            def splits(g, gp, reuse):
                if reuse:
                    stacks_ready(pool, g - 1, (gp - 1) % RING)
                split(g, k32, kpart, krest, k_masked, k_split)
                split(g, q32, qpart, qrest, q_copied, q_split)

            def invert_root(part):
                first, end = LN_PARTS[part]
                pool.wait_ge(ln_var, part + 1)
                nc.gpsimd.tensor_tensor(rstd[:, first:end], var_eps[:, first:end],
                                        minus_half[:, 0:1].to_broadcast([P, end - first]), ALU.pow).then_inc(ln_rstd, 1)

            invert_root(0)
            splits(0, 0, False)
            invert_root(1)
            splits(1, 1, True)
            with pool.Fori(0, LOOPED // RING) as it:
                for gp in range(RING):
                    splits(RING * it + gp + 2, (gp + 2) % RING, True)
            for part in (2, 3):
                invert_root(part)
            pool.wait_ge(router_steps, ROUTER_STEPS)
            pool.wait_ge(rows_copied, GROUPS)
            for b in range(BATCH):
                for k in range(TOPK):
                    nc.gpsimd.indirect_dma_start(
                        out=dispatch_d, out_offset=bass.IndirectOffsetOnAxis(ap=row_i[:, k, b:b + 1], axis=0),
                        in_=rows_out[:, b, k, :], in_offset=None).then_inc(rows_sent, 16)
            pool.wait_ge(table_steps, PADS_STEP)
            for e in range(EXPERTS):
                nc.gpsimd.indirect_dma_start(
                    out=dispatch_d, out_offset=bass.IndirectOffsetOnAxis(ap=pad_at[:, e:e + 1], axis=0),
                    in_=pad_row, in_offset=None).then_inc(pads_sent, 16)

            def store_tile(t, r, first=False):
                if not first:
                    pool.wait_ge(wait_taken, t)
                pool.wait_ge(y_gated, t + 1)
                nc.gpsimd.tensor_tensor(wait_taker[:], zero[:], zero[:], ALU.add).then_inc(wait_taken, 1)
                nc.gpsimd.indirect_dma_start(
                    out=result_d, out_offset=bass.IndirectOffsetOnAxis(ap=xg[r][:, D + 1:D + 2].bitcast(U32), axis=0),
                    in_=y_out[r], in_offset=None, bounds_check=TOPK * TOKENS - 1,
                    oob_is_err=False).then_inc(y_sent[r], 16)

            store_tile(0, 0, True)
            with pool.Fori(0, LOOPED_TILES // TRING) as it:
                for j in range(TRING):
                    store_tile(TRING * it + j + 1, (j + 1) % TRING)
            for t in range(1 + LOOPED_TILES, TILES):
                store_tile(t, t % TRING)

        @block.scalar
        def _(act):
            def copy_xqt(g, first=False):
                act.wait_ge(xqt_done, g + 1)
                if not first:
                    act.wait_ge(q_done, g)
                nc.scalar.activation(xq_t[:], prep[:], ACT.Copy).then_inc(xqt_copied, 1)

            def copy_q(g, first=False):
                act.wait_ge(q_done, g + 1)
                if not first:
                    act.wait_ge(q_split, 4 * g)
                nc.scalar.activation(q32[:], prep[:], ACT.Copy).then_inc(q_copied, 1)

            def copy_v(g, gp, first=False):
                act.wait_ge(v_done, g + 1)
                if not first:
                    act.wait_ge(attn_done, 4 * (g - 1))
                nc.scalar.activation(values[gp][:, :, :, 0:HD],
                                     prep[:].rearrange("p (b h d) -> p b h d", b=GB, d=HD),
                                     ACT.Copy).then_inc(v_copied, 1)

            def copy_shift(n, b, first=False):
                act.wait_ge(shift_turned, n + 1)
                if not first:
                    act.wait_ge(shift_loaded[b % 2], 16 * ((n - b % 2) // 2))
                nc.scalar.activation(shift_t[b % 2][:], shift_ps[0:3 * HEADS, 0:SEQ], ACT.Copy).then_inc(shift_copied, 1)

            def copy_attn(n):
                act.wait_ge(attn_done, n + 1 + CREDIT)
                act.wait_ge(heads_done, n + CREDIT)
                nc.scalar.activation(attn_t[:], attn_ps, ACT.Copy).then_inc(attn_copied, 1)

            def exp(n, np_, u, free):
                act.wait_ge(sexp_done, 2 * n + u + 1)
                if free:
                    act.wait_ge(attn_done, n - 1 + CREDIT)
                w = HEADS * SEQ // 2
                nc.scalar.activation(probs[np_][:, u * w:(u + 1) * w],
                                     sexp[u][:].rearrange("p i h q -> p (i h q)"), ACT.Exp).then_inc(exp_done, 1)

            def copy_yt(n):
                act.wait_ge(yt_done, n + 1)
                act.wait_ge(proj_done, n + CREDIT)
                nc.scalar.activation(y_t[:], prep[:, 0:SEQ], ACT.Copy).then_inc(yt_copied, 1)

            act.wait_ge(values_set, RING)
            for g in range(2):
                copy_xqt(g, g == 0)
                copy_q(g, g == 0)
            copy_v(0, 0, True)
            for b in range(GB - 1):
                copy_shift(b, b, b < 2)
            for u in range(2):
                exp(0, 0, u, False)

            def copy_normed(g):
                part = slice(GB * g, GB * (g + 1))
                act.wait_ge(xqt_done, GROUPS + g + 1)
                if g >= 2:
                    act.wait_ge(logits_done, g - 1)
                nc.scalar.activation(normed_t[g % 2], normed_ps[g % 2], ACT.Copy).then_inc(xqt_copied, 1)
                nc.scalar.activation(rows_out[:, part, 1, 0:D], rows_out[:, part, 0, 0:D], ACT.Copy).then_inc(rows_copied, 1)

            def group(g, gp, next_group, second_next):
                for b in range(GB):
                    n = GB * g + b
                    more = b < GB - 1 or next_group
                    copy_yt(n)
                    copy_attn(n)
                    if more:
                        exp(n + 1, (b + 1) % 2, 0, True)
                    if b == 0 or next_group:
                        copy_shift(n + 3, (b + 3) % GB)
                    if more:
                        exp(n + 1, (b + 1) % 2, 1, True)
                    if b == 1 and second_next:
                        copy_xqt(g + 2)
                    if b == 1 and second_next:
                        copy_q(g + 2)
                    if b == 2 and next_group:
                        copy_v(g + 1, (gp + 1) % RING)
                    for turned in TURNED.get(b, ()) if not next_group else ():
                        copy_normed(turned)

            with act.Fori(0, LOOPED // RING) as it:
                for gp in range(RING):
                    group(RING * it + gp, gp, True, True)
            group(GROUPS - 2, 0, True, False)
            group(GROUPS - 1, 1, False, False)

            copy_yt(BATCH)
            for g in LATE:
                copy_normed(g)
            act.wait_ge(router_steps, GAP_STEP)
            nc.scalar.activation(ratio, gap, ACT.Exp).then_inc(ratio_done, 1)

            def copy_xg(t, i):
                act.wait_ge(xg_turned, t + 1)
                nc.scalar.activation(xg_t[i], xg_ps[i], ACT.Copy).then_inc(xg_copied, 1)

            def gelu(t, i):
                act.wait_ge(hidden_turned, t + 1)
                nc.scalar.activation(hidden[i], turned_ps[i], ACT.Gelu).then_inc(gelu_done, 1)

            def gate_y(t, i, r):
                act.wait_ge(y_summed, t + 1)
                nc.scalar.activation(y_out[r], y_sum[i], ACT.Copy, scale=xg[r][:, D:D + 1]).then_inc(y_gated, 1)

            def tile_step(t, j):
                copy_xg(t + 1, (j + 1) % 2)
                gelu(t, j % 2)
                gate_y(t - 1, (j + 1) % 2, (j - 1) % TRING)

            copy_xg(0, 0)
            copy_xg(1, 1)
            gelu(0, 0)
            with act.Fori(0, LOOPED_TILES // TRING) as it:
                for j in range(TRING):
                    tile_step(TRING * it + j + 1, j + 1)
            for t in range(1 + LOOPED_TILES, TILES):
                tile_step(t, t)
            gate_y(TILES - 1, (TILES - 1) % 2, (TILES - 1) % TRING)

        @block.tensor
        def _(pe):
            def turn_xq(g):
                pe.wait_ge(xq_ready, GB * (g + 1))
                for b in range(GB):
                    last = nc.tensor.transpose(prep[:, b * SEQ:(b + 1) * SEQ], xq[:, b, :], ident[:])
                last.then_inc(xqt_done, 1)

            def project_q(g):
                pe.wait_ge(xqt_copied, g + 1)
                nc.tensor.matmul(prep[:], wq_sb[:], xq_t[:], start=True, stop=True).then_inc(q_done, 1)

            def project_k(g, gp):
                ctx_ready(pe, g, gp)
                nc.tensor.matmul(prep[:], wkv_sb[:, 0:D], ctx_sb[gp][:], start=True, stop=True).then_inc(k_done, 1)

            def project_v(g, gp):
                for b in range(GB):
                    last = nc.tensor.matmul(prep[:, b * D:(b + 1) * D], ctx_sb[gp][:, b * SEQ:(b + 1) * SEQ],
                                            wkv_sb[:, D:2 * D], start=True, stop=True)
                last.then_inc(v_done, 1)

            def turn_shift(n, b):
                pe.wait_ge(shift_split, 4 * (n + 1))
                nc.tensor.transpose(shift_ps[0:SHIFT_COLS * HEADS, 0:SEQ], shift[b % 2][:].rearrange("p s c -> p (s c)"),
                                    ident_b[:]).then_inc(shift_turned, 1)

            def scores_for_max(g, gp, j, free):
                b, u = divmod(j, UNITS)
                if free or j >= 2:
                    pe.wait_ge(max_taken, 4 * UNITS * g + j - 1)
                ks = slice(b * SEQ, (b + 1) * SEQ)
                for i in range(2):
                    for hp in range(2):
                        last = nc.tensor.matmul(smax[j % 2][:, i, hp, :], qstack[gp][0:ROWS, 2 * u + i, hp, ks],
                                                kstack[gp][0:ROWS, 2 * u + i, ks], start=True, stop=True)
                last.then_inc(smax_done, 1)

            def scores_for_exp(n, b, gp, u, free):
                if free:
                    pe.wait_ge(exp_done, 2 * n + u - 1)
                ks = slice(b * SEQ, (b + 1) * SEQ)
                for i in range(4):
                    last = nc.tensor.matmul(sexp[u][:, i, :, :], kstack[gp][0:ROWS, 4 * u + i, ks],
                                            qstack[gp][0:ROWS, 4 * u + i, :, ks], start=True, stop=True)
                last.then_inc(sexp_done, 1)

            def attend(n, b, gp):
                pe.wait_ge(exp_done, 2 * n + 2)
                pe.wait_ge(y_ready, n + 1)
                for h in range(HEADS):
                    rows = slice(HEADROOM * (h % 4), HEADROOM * (h % 4 + 1))
                    last = nc.tensor.matmul(attn_ps[rows, h // 4, :], values[gp][:, b, h, :],
                                            probs[b % 2][:, h * SEQ:(h + 1) * SEQ], start=True, stop=True)
                last.then_inc(attn_done, 1)

            def turn_heads(n):
                pe.wait_ge(attn_copied, n + 1)
                for c in range(HEADS // 4):
                    last = nc.tensor.transpose(tail[:, c * P:(c + 1) * P], attn_t[:, c, :], ident[:])
                last.then_inc(heads_done, 1)

            def turn_y(n):
                pe.wait_ge(y_ready, n + 1)
                nc.tensor.transpose(prep[:, 0:SEQ], y[:].rearrange("p h d -> p (h d)"), ident[:]).then_inc(yt_done, 1)

            def project_y(n):
                pe.wait_ge(yt_copied, n + 1)
                nc.tensor.matmul(prep[:, 0:D], y_t[:], wc_sb[:], start=True, stop=True).then_inc(proj_done, 1)

            def project_router(g):
                pe.wait_ge(xqt_copied, GROUPS + g + 1)
                for b in range(GB):
                    n = GB * g + b
                    last = nc.tensor.matmul(logits_ps[:, n * EXPERTS:(n + 1) * EXPERTS], normed_t[g % 2][:, b * SEQ:(b + 1) * SEQ],
                                            router_sb[:], start=True, stop=True)
                last.then_inc(logits_done, 1)

            def turn_rows(g, finished):
                pe.wait_ge(rows_normed, GB * (g + 1))
                if g >= 2:
                    pe.wait_ge(xqt_copied, GROUPS + g - 1)
                if g % 2 == 0:
                    pe.wait_ge(resid_done, finished + CREDIT)
                for b in range(GB):
                    last = nc.tensor.transpose(normed_ps[g % 2][:, b * SEQ:(b + 1) * SEQ], rows_out[:, GB * g + b, 0, 0:D],
                                               ident[:])
                last.then_inc(xqt_done, 1)
                if g:
                    project_router(g - 1)

            for begun in (attn_done, heads_done, proj_done):
                pe.sem_inc(begun, CREDIT)
            pe.wait_ge(weights_loaded, 48)
            pe.wait_ge(ident_made, 2)
            for g in range(2):
                if g:
                    pe.wait_ge(q_copied, g)
                project_k(g, g)
                pe.wait_ge(k_masked, g + 1)
                turn_xq(g)
                project_q(g)
            pe.wait_ge(q_copied, 2)
            project_v(0, 0)
            stacks_ready(pe, 0, 0)
            for b in range(GB):
                for u in range(UNITS):
                    scores_for_max(0, 0, UNITS * b + u, False)
                if b:
                    pe.wait_ge(v_copied, 1) if b == 1 else pe.wait_ge(shift_copied, b - 1)
                    turn_shift(b - 1, b - 1)
            pe.wait_ge(shift_loaded[0], 16)
            for u in range(2):
                scores_for_exp(0, 0, 0, u, False)

            def group(g, gp, next_group, second_next):
                ahead, two_ahead = (gp + 1) % RING, (gp + 2) % RING
                for b in range(GB):
                    n = GB * g + b
                    more = b < GB - 1 or next_group
                    ngp, nb = (gp, b + 1) if b < GB - 1 else (ahead, 0)
                    if b == 0:
                        pe.wait_ge(shift_copied, n + 3)
                    elif b == 1 and second_next:
                        pe.wait_ge(k_masked, g + 3)
                    elif b == 2 and second_next:
                        pe.wait_ge(q_copied, g + 3)
                    elif b == 3 and next_group:
                        pe.wait_ge(v_copied, g + 2)
                    elif next_group or b == 1:
                        pe.wait_ge(shift_copied, n + 3)
                    else:
                        pe.wait_ge(xqt_copied, GROUPS + TURNED[b - 1][-1] // 2 * 2 + 1)
                    turn_y(n)
                    attend(n, b, gp)
                    if more:
                        pe.wait_ge(shift_loaded[nb % 2], 16 * ((n + 1 - nb % 2) // 2 + 1))
                        scores_for_exp(n + 1, nb, ngp, 0, True)
                    if next_group:
                        if b == 0:
                            stacks_ready(pe, g + 1, ahead)
                        scores_for_max(g + 1, ahead, UNITS * b, True)
                    project_y(n)
                    if next_group:
                        scores_for_max(g + 1, ahead, UNITS * b + 1, True)
                    turn_heads(n)
                    if b == 0 or next_group:
                        pe.wait_ge(resid_done, n + 1)
                        turn_shift(n + 3, (b + 3) % GB)
                    if more:
                        scores_for_exp(n + 1, nb, ngp, 1, True)
                    if next_group:
                        scores_for_max(g + 1, ahead, UNITS * b + 2, True)
                    if b < 2 and second_next or b == 2 and next_group:
                        pe.wait_ge(shift_copied, n + 4)
                    if b == 0 and second_next:
                        project_k(g + 2, two_ahead)
                    if b == 1 and second_next:
                        turn_xq(g + 2)
                    if b == 2 and next_group:
                        project_v(g + 1, ahead)
                    if next_group:
                        scores_for_max(g + 1, ahead, UNITS * b + 3, True)
                    if b == 1 and second_next:
                        project_q(g + 2)
                    if b == 1 and not next_group:
                        pe.wait_ge(ffn_loaded, 16 * (1 + 2 * EXPERTS))
                    for turned in TURNED.get(b, ()) if not next_group else ():
                        turn_rows(turned, n)

            with pe.Fori(0, LOOPED // RING) as it:
                for gp in range(RING):
                    group(RING * it + gp, gp, True, True)
            group(GROUPS - 2, 0, True, False)
            group(GROUPS - 1, 1, False, False)

            pe.wait_ge(xqt_copied, GROUPS + LATE[0])
            turn_y(BATCH)
            project_y(BATCH)
            for g in LATE:
                turn_rows(g, BATCH)
            project_router(GROUPS - 1)
            pe.wait_ge(router_steps, PICKED_STEP)
            all_picked = picked.rearrange("p b e -> p (b e)")
            nc.tensor.matmul(before_ps, before[:], all_picked, start=True, stop=True)
            nc.tensor.matmul(count_ps, ones_b[:], all_picked, start=True, stop=True).then_inc(ranks_done, 1)

            def turn_tile(t, i, r, first=False):
                pe.wait_ge(xg_loaded[r], ring_count(t, r))
                if not first:
                    pe.wait_ge(xg_copied, t)
                nc.tensor.transpose(xg_ps[i], xg[r][:, 0:D], ident[:]).then_inc(xg_turned, 1)

            def up(t, i, e):
                pe.wait_ge(xg_copied, t + 1)
                nc.tensor.matmul(up_ps[i], xg_t[i], w1_sb[:].rearrange("p e f -> p (e f)")[:, bass.ds(e * FF, FF)],
                                 start=True, stop=True).then_inc(up_done, 1)

            def turn_hidden(t, i):
                pe.wait_ge(bias_added, t + 1)
                for c in range(FC):
                    last = nc.tensor.transpose(turned_ps[i][:, c * P:(c + 1) * P], biased[i][:, c * P:(c + 1) * P], ident[:])
                last.then_inc(hidden_turned, 1)

            def down(t, i, e):
                pe.wait_ge(gelu_done, t + 1)
                for c in range(FC):
                    last = nc.tensor.matmul(down_ps[i], hidden[i][:, c * P:(c + 1) * P],
                                            w2_sb[:].rearrange("p e c d -> p (e c d)")[:, bass.ds(e * FF + c * D, D)],
                                            start=(c == 0), stop=(c == FC - 1))
                last.then_inc(down_done, 1)

            def expert_reg(t):
                return pe.value_load(expert_of[0:1, bass.ds(t, 1)], min_val=0, max_val=EXPERTS - 1)

            def tile_steps(first, js):
                before_e, e = expert_reg(first + js[0] - 1), expert_reg(first + js[0])
                for j in js:
                    t = first + j
                    up(t, j % 2, e)
                    turn_tile(t + 1, (j + 1) % 2, (j + 1) % TRING)
                    down(t - 1, (j + 1) % 2, before_e)
                    before_e, e = e, (expert_reg(t + 1) if j != js[-1] else None)
                    turn_hidden(t, j % 2)

            pe.wait_ge(table_steps, TABLE_STEPS)
            turn_tile(0, 0, 0, True)
            up(0, 0, expert_reg(0))
            turn_tile(1, 1, 1, True)
            turn_hidden(0, 0)
            with pe.Fori(0, LOOPED_TILES // TRING) as it:
                tile_steps(TRING * it, range(1, TRING + 1))
            tile_steps(0, range(1 + LOOPED_TILES, TILES))
            down(TILES - 1, (TILES - 1) % 2, expert_reg(TILES - 1))

        @block.vector
        def _(dve):
            steps = [0]

            def step(ins):
                steps[0] += 1
                ins.then_inc(mask_prep, 1)

            nc.vector.memset(y[:], 0.0).then_inc(y_ready, 1)
            nc.vector.memset(xs_all[:, 0, :], 0.0).then_inc(shift_cleared, 1)
            dve.wait_ge(masks_loaded, 32)
            step(nc.vector.tensor_copy(mask_rows[:], mask_rows8[:]))
            step(nc.vector.tensor_scalar(mask_cols[:], mask_cols8[:], float(HD) ** -0.5, None, ALU.mult))
            step(nc.vector.memset(key_terms[:, 3:6, :], 1.0))
            step(nc.vector.memset(query_terms[:, 3:6, :], 0.0))
            dve.wait_ge(mask_prep, 4)
            for i in range(2):
                nc.vector.memset(shift[i][:], 0.0).then_inc(shift_cleared, 1)
            for s in range(3):
                step(nc.vector.tensor_scalar(key_terms[:, s, :], mask_rows[:], -neg[s], neg[s], ALU.mult, ALU.add))
                step(nc.vector.tensor_copy(query_terms[:, s, :], mask_rows[:]))

            def clear_stack(i):
                nc.vector.memset(stacks[:, q_at[i]:q_at[i] + QW].bitcast(U32), 0).then_inc(cleared, 1)

            def row_stats(batches):
                for n in batches:
                    nc.vector.bn_stats(stats[:, n, :], xs[:, n, :]).then_inc(ln_stats, 1)

            def row_moments(part):
                at = slice(*LN_PARTS[part])
                dve.wait_ge(ln_stats, BATCH * (part // 2) + at.stop)
                nc.vector.tensor_tensor(mean_sum[:, at], stats[:, at, 1], stats[:, at, 4], ALU.add).then_inc(ln_moments, 1)
                nc.vector.tensor_tensor(mean_diff[:, at], stats[:, at, 1], stats[:, at, 4], ALU.subtract).then_inc(ln_moments, 1)
                nc.vector.tensor_tensor(moment_sum[:, at], stats[:, at, 2], stats[:, at, 5], ALU.add).then_inc(ln_moments, 1)
                dve.wait_ge(ln_moments, 6 * part + 3)
                nc.vector.tensor_scalar(mean[:, at], mean_sum[:, at], 0.5, None, ALU.mult).then_inc(ln_moments, 1)
                nc.vector.scalar_tensor_tensor(out=diff_sq[:, at], in0=mean_diff[:, at], scalar=0.25, in1=mean_diff[:, at],
                                               op0=ALU.mult, op1=ALU.mult).then_inc(ln_moments, 1)
                nc.vector.tensor_scalar(moment_sum[:, at], moment_sum[:, at], 1.0 / D, EPS,
                                        ALU.mult, ALU.add).then_inc(ln_moments, 1)
                dve.wait_ge(ln_moments, 6 * part + 6)
                nc.vector.tensor_tensor(var_eps[:, at], moment_sum[:, at], diff_sq[:, at], ALU.add).then_inc(ln_var, 1)

            def scale_queries(part):
                at = slice(*LN_PARTS[part])
                dve.wait_ge(ln_rstd, part + 1)
                nc.vector.tensor_tensor(qscale[:, at], rstd[:, at], mask_cols[:, at], ALU.mult).then_inc(ln_scale, 1)
                dve.wait_ge(ln_scale, part + 1)

            def layernorm_apply(g, first=False):
                if not first:
                    dve.wait_ge(xqt_done, g)
                for b in range(GB):
                    n = GB * g + b
                    one = slice(n, n + 1) if isinstance(n, int) else bass.ds(n, 1)
                    nc.vector.tensor_scalar(xq[:, b, :], xs[:, n, :], mean[:, one], qscale[:, one],
                                            ALU.subtract, ALU.mult).then_inc(xq_ready, 1)

            def mask_k(g, gp, first=False):
                dve.wait_ge(k_done, g + 1)
                ctx_ready(dve, g, gp)
                if not first:
                    dve.wait_ge(k_split, 4 * g)
                nc.vector.tensor_tensor(k32[:], prep[:], kmask[gp][:], ALU.mult).then_inc(k_masked, 1)

            def take_max(g, j):
                b, u = divmod(j, UNITS)
                dve.wait_ge(smax_done, 4 * UNITS * g + j + 1)
                dst = negmax[:, 2 * u:2 * u + 2, :]
                nc.vector.tensor_reduce(dst, smax[j % 2][:], AX.X, ALU.max, negate=True).then_inc(max_taken, 1)

            def split_shift(n, b, first=False):
                dve.wait_ge(max_taken, UNITS * (n + 1))
                if not first:
                    dve.wait_ge(shift_turned, n - 1)
                src = negmax[:].rearrange("p i h -> p (i h)")
                part = shift[b % 2]
                nc.vector.tensor_copy(part[:, 0, :], src).then_inc(shift_split, 1)
                dve.wait_ge(shift_split, 4 * n + 1)
                nc.vector.tensor_tensor(shift_rest[:], src, part[:, 0, :], ALU.subtract).then_inc(shift_split, 1)
                dve.wait_ge(shift_split, 4 * n + 2)
                nc.vector.tensor_copy(part[:, 1, :], shift_rest[:]).then_inc(shift_split, 1)
                dve.wait_ge(shift_split, 4 * n + 3)
                nc.vector.tensor_tensor(part[:, 2, :], shift_rest[:], part[:, 1, :], ALU.subtract).then_inc(shift_split, 1)

            def normalise(n):
                dve.wait_ge(heads_done, n + 1 + CREDIT)
                nc.vector.reciprocal(denom[:], heads_ps[:, :, HD]).then_inc(denom_done, 1)
                dve.wait_ge(denom_done, n + 1)
                dve.wait_ge(yt_done, n + 1)
                nc.vector.tensor_tensor(y[:], heads_ps[:, :, 0:HD],
                                        denom[:].rearrange("p (h o) -> p h o", o=1).to_broadcast([P, HEADS, HD]),
                                        ALU.mult).then_inc(y_ready, 1)

            def residual(n):
                dve.wait_ge(proj_done, n + 1 + CREDIT)
                nc.vector.tensor_tensor(xs_all[:, n, :], xs_all[:, n, :], prep[:, 0:D], ALU.add).then_inc(resid_done, 1)

            dve.wait_ge(x_loaded, 16)
            row_stats(range(2 * GB))
            row_moments(0)
            clear_stack(0)
            scale_queries(0)
            layernorm_apply(0, True)
            mask_k(0, 0, True)
            clear_stack(1)
            layernorm_apply(1)
            mask_k(1, 1)
            dve.wait_ge(x_rest_loaded, 16)
            row_stats(range(2 * GB, BATCH))
            row_moments(1)
            clear_stack(2)
            scale_queries(1)
            dve.wait_ge(shift_cleared, 3)
            for b in range(GB):
                for u in range(UNITS):
                    take_max(0, UNITS * b + u)
                split_shift(b, b, b < 2)

            def norm_row(n):
                nc.vector.tensor_scalar(rows_out[:, n, 0, 0:D], xs[:, n, :], mean[:, n:n + 1], rstd[:, n:n + 1],
                                        ALU.subtract, ALU.mult).then_inc(rows_normed, 1)

            def group(g, gp, next_group, second_next):
                for b in range(GB):
                    n = GB * g + b
                    if next_group:
                        take_max(g + 1, UNITS * b)
                    residual(n)
                    if next_group:
                        take_max(g + 1, UNITS * b + 1)
                    normalise(n)
                    if not next_group:
                        for row in APPLIED.get(b, ()):
                            norm_row(row)
                    if next_group:
                        take_max(g + 1, UNITS * b + 2)
                        if b == 0 and second_next:
                            mask_k(g + 2, (gp + 2) % RING)
                        take_max(g + 1, UNITS * b + 3)
                        split_shift(n + GB, b)
                    if next_group and not second_next:
                        dve.wait_ge(resid_done, GB * (GROUPS - 2) + CREDIT)
                        row_stats(range(6 * b, 6 * b + 6))
                    if b == 0 and not next_group:
                        dve.wait_ge(resid_done, EARLY + CREDIT)
                        row_stats(range(GB * (GROUPS - 2), EARLY))
                        row_moments(2)
                        dve.wait_ge(ln_rstd, 3)
                    if b == 0 and second_next:
                        layernorm_apply(g + 2)

            with dve.Fori(0, LOOPED // RING) as it:
                for gp in range(RING):
                    group(RING * it + gp, gp, True, True)
            group(GROUPS - 2, 0, True, False)
            group(GROUPS - 1, 1, False, False)
            assert steps[0] == 10

            table = [0]

            def link(ins):
                table[0] += 1
                ins.then_inc(table_steps, 1)
                dve.wait_ge(table_steps, table[0])

            routed = [0]

            def did(ins):
                routed[0] += 1
                ins.then_inc(router_steps, 1)
                dve.wait_ge(router_steps, routed[0])

            residual(BATCH)
            dve.wait_ge(resid_done, BATCH + CREDIT)
            row_stats(range(EARLY, BATCH))
            row_moments(3)
            for dst, src in ((first_row, first_row_i), (iota8, iota_i), (lane, lane_i), (tile_lim, tile_lim_i), (tile_no, tile_no_i)):
                link(nc.vector.tensor_copy(dst, src[:]))
            link(nc.vector.memset(pad_row, 0.0))
            link(nc.vector.memset(pad_row[:, D + 1:D + 2].bitcast(I32), DROPPED))
            assert table[0] == DUMMY_STEP
            dve.wait_ge(ln_rstd, 4)
            for n in range(EARLY, BATCH):
                norm_row(n)

            def wide(t):
                return t.rearrange("p (b o) -> p b o", o=1).to_broadcast([P, BATCH, EXPERTS])

            ids = iota8.rearrange("p (o e) -> p o e", o=1).to_broadcast([P, BATCH, EXPERTS])
            dve.wait_ge(logits_done, GROUPS)
            did(nc.vector.tensor_copy(logits, logits_ps.rearrange("p (b e) -> p b e", b=BATCH)))
            for k, src in enumerate((logits, masked)):
                did(nc.vector.tensor_reduce(top[k], src, AX.X, ALU.max))
                if k:
                    did(nc.vector.tensor_tensor(gap, top[1], top[0], ALU.subtract))
                    assert routed[0] == GAP_STEP, routed[0]
                did(nc.vector.tensor_tensor(tmp8, src, wide(top[k]), ALU.is_equal))
                did(nc.vector.scalar_tensor_tensor(out=tmp8, in0=tmp8, scalar=-float(EXPERTS), in1=ids,
                                                   op0=ALU.mult, op1=ALU.add))
                did(nc.vector.tensor_reduce(index, tmp8, AX.X, ALU.min))
                did(nc.vector.scalar_tensor_tensor(out=chosen[k], in0=ids, scalar=-float(EXPERTS), in1=wide(index),
                                                   op0=ALU.add, op1=ALU.is_equal))
                if not k:
                    did(nc.vector.scalar_tensor_tensor(out=masked, in0=chosen[0], scalar=-3.0e38, in1=logits,
                                                       op0=ALU.mult, op1=ALU.add))
            did(nc.vector.tensor_tensor(picked, chosen[0], chosen[1], ALU.add))
            assert routed[0] == PICKED_STEP, routed[0]
            dve.wait_ge(ratio_done, 1)
            did(nc.vector.tensor_scalar(index, ratio, 1.0, None, ALU.add))
            did(nc.vector.reciprocal(share[0], index))
            did(nc.vector.tensor_tensor(share[1], share[0], ratio, ALU.mult))
            for k in range(TOPK):
                did(nc.vector.tensor_copy(rows_out[:, :, k, D], share[k]))
                did(nc.vector.tensor_copy(rows_out[:, :, k, D + 1].bitcast(I32), place_i[:, k, :]))
            dve.wait_ge(ranks_done, 1)
            totals = (totals_a, totals_b)
            did(nc.vector.tensor_copy(totals_a, count_ps.rearrange("p (b e) -> p b e", b=BATCH)))
            for n in range(SCAN_STEPS):
                hop, a, b = 1 << n, totals[n % 2], totals[(n + 1) % 2]
                did(nc.vector.tensor_copy(b[:, 0:hop, :], a[:, 0:hop, :]))
                did(nc.vector.tensor_tensor(b[:, hop:, :], a[:, hop:, :], a[:, 0:BATCH - hop, :], ALU.add))
            total, rank = totals[SCAN_STEPS % 2], totals[(SCAN_STEPS + 1) % 2]
            did(nc.vector.tensor_tensor(rank[:, 0, :], before_ps[:, 0:EXPERTS], first_row, ALU.add))
            did(nc.vector.tensor_tensor(rank[:, 1:, :], total[:, 0:BATCH - 1, :],
                                        first_row.rearrange("p (o e) -> p o e", o=1).to_broadcast([P, BATCH - 1, EXPERTS]),
                                        ALU.add))
            did(nc.vector.tensor_tensor(rank[:, 1:, :], rank[:, 1:, :],
                                        before_ps[:, EXPERTS:].rearrange("p (b e) -> p b e", e=EXPERTS), ALU.add))
            for k in range(TOPK):
                did(nc.vector.tensor_tensor(chosen[k], chosen[k], rank, ALU.mult))
                did(nc.vector.tensor_reduce(row_f[:, k * BATCH:(k + 1) * BATCH], chosen[k], AX.X, ALU.add))
            did(nc.vector.tensor_copy(row_i.rearrange("p k b -> p (k b)"), row_f))
            assert routed[0] == ROUTER_STEPS, routed[0]

            link(nc.vector.tensor_tensor(last_row, total[:, BATCH - 1, :], first_row, ALU.add))
            link(nc.vector.tensor_scalar(row_pad, last_row, lane, None, ALU.add))
            link(nc.vector.tensor_copy(pad_at, row_pad))
            assert table[0] == PADS_STEP
            link(nc.vector.tensor_tensor(used, last_row[0:1, :], first_row[0:1, :], ALU.subtract))
            link(nc.vector.tensor_tensor(over, used.rearrange("p (e o) -> p e o", o=1).to_broadcast([1, EXPERTS, TOKENS // P]),
                                         tile_lim.rearrange("p (o j) -> p o j", o=1).to_broadcast([1, EXPERTS, TOKENS // P]),
                                         ALU.is_gt))
            link(nc.vector.tensor_reduce(tiles, over, AX.X, ALU.add))
            link(nc.vector.tensor_copy(ends[0], tiles))
            for n, hop in enumerate((1, 2, 4)):
                a, b = ends[n % 2], ends[(n + 1) % 2]
                link(nc.vector.tensor_copy(b[:, 0:hop], a[:, 0:hop]))
                link(nc.vector.tensor_tensor(b[:, hop:], a[:, hop:], a[:, 0:EXPERTS - hop], ALU.add))
            wide_no = tile_no.rearrange("p (t o) -> p t o", o=1).to_broadcast([1, TABLE, EXPERTS])

            def by_expert(t):
                return t.rearrange("p (o e) -> p o e", o=1).to_broadcast([1, TABLE, EXPERTS])

            link(nc.vector.tensor_tensor(passed, wide_no, by_expert(ends[1]), ALU.is_ge))
            link(nc.vector.tensor_reduce(expert_f, passed, AX.X, ALU.add))
            link(nc.vector.tensor_tensor(passed2, passed, by_expert(tiles), ALU.mult))
            link(nc.vector.tensor_reduce(tile_f[0], passed2, AX.X, ALU.add))
            link(nc.vector.tensor_tensor(tile_f[1], tile_no, tile_f[0], ALU.subtract))
            link(nc.vector.tensor_scalar(tile_f[2], expert_f, float(EXPERTS), float(P), ALU.is_lt, ALU.mult))
            link(nc.vector.tensor_tensor(tile_f[0], tile_f[1], tile_f[2], ALU.mult))
            link(nc.vector.scalar_tensor_tensor(out=tile_f[1], in0=expert_f, scalar=float(REGION), in1=tile_f[0],
                                                op0=ALU.mult, op1=ALU.add))
            link(nc.vector.tensor_copy(start_of, tile_f[1]))
            link(nc.vector.tensor_scalar(tile_f[2], expert_f, float(EXPERTS - 1), None, ALU.min))
            link(nc.vector.tensor_copy(expert_of, tile_f[2]))
            assert table[0] == TABLE_STEPS, table[0]

            def expert_reg(t):
                return dve.value_load(expert_of[0:1, bass.ds(t, 1)], min_val=0, max_val=EXPERTS - 1)

            def add_bias(t, i, e):
                dve.wait_ge(up_done, t + 1)
                nc.vector.tensor_tensor(biased[i], up_ps[i], b1_sb[:, bass.ds(e * FF, FF)], ALU.add).then_inc(bias_added, 1)

            def sum_y(t, i, e):
                dve.wait_ge(down_done, t + 1)
                nc.vector.tensor_tensor(y_sum[i], down_ps[i], b2_sb[:, bass.ds(e * D, D)], ALU.add).then_inc(y_summed, 1)

            def tile_step(t, j):
                add_bias(t, j % 2, expert_reg(t))
                sum_y(t - 1, (j + 1) % 2, expert_reg(t - 1))

            dve.wait_ge(bias_loaded, 32)
            add_bias(0, 0, expert_reg(0))
            with dve.Fori(0, LOOPED_TILES // TRING) as it:
                for j in range(TRING):
                    tile_step(TRING * it + j + 1, j + 1)
            for t in range(1 + LOOPED_TILES, TILES):
                tile_step(t, t)
            sum_y(TILES - 1, (TILES - 1) % 2, expert_reg(TILES - 1))
            for g in range(GROUPS):
                part = slice(GB * g, GB * (g + 1))
                dve.wait_ge(found_loaded[g], 32)
                for k in range(TOPK):
                    nc.vector.tensor_tensor(xs[:, part, :], xs[:, part, :], found[k][:, part, :], ALU.add).then_inc(found_added, 1)
                    if not k:
                        dve.wait_ge(found_added, 2 * g + 1)


def kernel(x, ctx_1024, mask_BxS2_bf1, L0_xattn_Wq, L0_xattn_Wkv, L0_xattn_Wc, L0_ffn_router_w, L0_ffn_w1, L0_ffn_b1,
           L0_ffn_w2, L0_ffn_b2):
    import numpy as np
    import concourse.bacc as bacc
    from concourse import mybir as mb
    from concourse.bass_utils import run_bass_kernel_spmd

    def lay(a):
        return np.ascontiguousarray(a)

    def pair_columns(w_t):
        return w_t.reshape(D, PAIRS, 2, HD).transpose(0, 2, 3, 1).reshape(D, D)

    x, ctx = np.asarray(x), np.asarray(ctx_1024)
    mask = np.asarray(mask_BxS2_bf1).view(np.uint8)
    wkv_t = np.asarray(L0_xattn_Wkv).T
    arrays = {
        "x": lay(x.transpose(1, 0, 2)),
        "ctx_t": lay(ctx.transpose(2, 0, 1).reshape(D, BATCH * SEQ)),
        "mask": lay(mask.reshape(GROUPS, GT)),
        "mask_t": lay(mask.T),
        "wq_t": lay(pair_columns(np.asarray(L0_xattn_Wq).T)),
        "wkv_t": lay(np.concatenate([pair_columns(wkv_t[:, :D]), wkv_t[:, D:]], axis=1)),
        "wc_t": lay(np.asarray(L0_xattn_Wc).T),
        "router_t": lay(np.asarray(L0_ffn_router_w).T),
        "w1_t": lay(np.asarray(L0_ffn_w1).transpose(2, 0, 1)),
        "b1": lay(np.asarray(L0_ffn_b1).reshape(1, EXPERTS * FF)),
        "w2_t": lay(np.asarray(L0_ffn_w2).reshape(EXPERTS, D, FC, P).transpose(3, 0, 2, 1)),
        "b2": lay(np.asarray(L0_ffn_b2).reshape(1, EXPERTS * D)),
    }
    nc = bacc.Bacc("TRN2", target_bir_lowering=False, num_devices=1)
    args = [nc.dram_tensor(f"{name}_dram", a.shape, mb.dt.from_np(a.dtype), kind="ExternalInput").ap()
            for name, a in arrays.items()]
    out = nc.dram_tensor("out_dram", (SEQ, BATCH, D), mb.dt.float32, kind="ExternalOutput").ap()
    xattn_ffn(nc, *args, out)
    r = run_bass_kernel_spmd(nc, [{f"{name}_dram": a for name, a in arrays.items()}], core_ids=[0])
    return r.results[0]["out_dram"].transpose(1, 0, 2)
```
